# Optimizing a Trainium2 kernel written in Bass

```python
import numpy as np
import jax
import jax.numpy as jnp

def _softmax(x, axis=-1):
    return jax.nn.softmax(x, axis=axis)

def _gelu(x):
    return jax.nn.gelu(x, approximate=True)

def _silu(x):
    return jax.nn.silu(x)

def _sigmoid(x):
    return jax.nn.sigmoid(x)

def _layernorm(x, axis=-1, eps=1e-05):
    m = jnp.mean(x, axis=axis, keepdims=True)
    v = jnp.var(x, axis=axis, keepdims=True)
    return (x - m) / jnp.sqrt(v + eps)

def _scatter_add(tgt, idx, src, axis=0):
    return tgt.at[idx].add(src)

def _segment_sum(src, seg, n):
    return jax.ops.segment_sum(src, seg, n)
kernel_name = 'mk_adaln_ffn_d1_seqx_r2_c5e9a0'

def setup_inputs(seed: int=0):
    np.random.seed(seed)
    _w = jnp.asarray

    def _rec_inputs():
        import jax
        import jax.numpy as jnp
        _rk = jax.random.key(seed)
        x = -0.000125 + 0.9999 * jax.random.normal(jax.random.fold_in(_rk, 1), (8, 512, 2048), jnp.float32)
        _lenS = 512 - jax.random.randint(jax.random.fold_in(_rk, 7), (8,), 0, max(1, 512 // 4) + 1, jnp.int32)
        _lenS2 = 512 - jax.random.randint(jax.random.fold_in(_rk, 8), (8,), 0, max(1, 512 // 4) + 1, jnp.int32)
        itok_B_6_15 = jax.random.randint(jax.random.fold_in(_rk, 11), (8,), 6, 16, jnp.int32)
        return (x, itok_B_6_15)
    x, itok_B_6_15 = _rec_inputs()

    def _L0_cond_setup():
        import jax, jax.numpy as jnp
        import numpy as np
        B, S, D_IN, D_OUT = (4, 1024, 2048, 2048)
        RANK, MAX_LORAS = (16, 32)
        key = jax.random.key(seed)
        ks = jax.random.split(key, 6)
        x = jax.random.normal(ks[0], (B, S, D_IN), dtype=jnp.float32)
        adapter_ids = jax.random.randint(ks[1], (B,), 0, MAX_LORAS)
        base_weight = jax.random.normal(ks[2], (D_OUT, D_IN), dtype=jnp.float32) * D_IN ** (-0.5)
        base_bias = jax.random.normal(ks[3], (D_OUT,), dtype=jnp.float32) * 0.01
        lora_A_w = jax.random.normal(ks[4], (MAX_LORAS, RANK, D_IN), dtype=jnp.float32) * D_IN ** (-0.5)
        lora_B_w = jax.random.normal(ks[5], (MAX_LORAS, D_OUT, RANK), dtype=jnp.float32) * RANK ** (-0.5)
        return {'x': x, 'adapter_ids': adapter_ids, 'base_weight': base_weight, 'base_bias': base_bias, 'lora_A_w': lora_A_w, 'lora_B_w': lora_B_w}
    _L0_cond_all = _L0_cond_setup()
    _L0_cond_in = {k: v for k, v in _L0_cond_all.items() if k in ('base_weight', 'base_bias', 'lora_A_w', 'lora_B_w')}
    del _L0_cond_all

    def _L0_ffn_setup():
        import jax, jax.numpy as jnp
        import numpy as np
        HID, BOT, RDIM, NSLOT, K, VB = (2048, 64, 48, 512, 8, 128)
        TAU_LOW, TAU_HIGH, EARLY_EXIT = (0.5, 2.0, 0.05)

        def _uncertainty(h, Wu1, bu1, Wu2, bu2):
            var = jnp.var(h, axis=-1)
            log_var = jnp.log1p(var)
            norm_var = log_var / (jnp.mean(log_var) + 1e-06)
            learned = (jax.nn.gelu(h @ Wu1.T + bu1) @ Wu2.T + bu2)[..., 0]
            return jnp.clip(norm_var * 0.5 + jax.nn.sigmoid(learned) * 2.5, 0.0, 5.0)
        key = jax.random.key(seed)
        ks = jax.random.split(key, 12)
        B, S = (2, 1024)
        return {'hidden_states': jax.random.normal(ks[0], (B, S, HID), dtype=jnp.float32), 'Wq': jax.random.normal(ks[1], (BOT, HID), dtype=jnp.float32) / np.sqrt(HID), 'Wr': jax.random.normal(ks[2], (RDIM, BOT), dtype=jnp.float32) / np.sqrt(BOT), 'aux_keys': jax.random.normal(ks[3], (NSLOT, BOT), dtype=jnp.float32) * 0.01, 'aux_values': jax.random.normal(ks[4], (NSLOT, HID), dtype=jnp.float32) * 0.02, 'Wvd': jax.random.normal(ks[5], (VB, HID), dtype=jnp.float32) * 0.1 / np.sqrt(HID), 'Wvu': jax.random.normal(ks[6], (HID, VB), dtype=jnp.float32) * 0.1 / np.sqrt(VB), 'Wu1': jax.random.normal(ks[7], (HID // 4, HID), dtype=jnp.float32) / np.sqrt(HID), 'bu1': jnp.zeros((HID // 4,), dtype=jnp.float32), 'Wu2': jax.random.normal(ks[8], (1, HID // 4), dtype=jnp.float32) * 0.01, 'bu2': jnp.zeros((1,), dtype=jnp.float32), 'gate_w1': jnp.float32(0.5), 'gate_bias': jnp.float32(-1.0), 'log_rel': jnp.zeros((NSLOT,), dtype=jnp.float32)}
    _L0_ffn_all = _L0_ffn_setup()
    _L0_ffn_in = {k: v for k, v in _L0_ffn_all.items() if k in ('Wq', 'Wr', 'aux_keys', 'aux_values', 'Wvd', 'Wvu', 'Wu1', 'bu1', 'Wu2', 'bu2', 'gate_w1', 'gate_bias', 'log_rel')}
    del _L0_ffn_all
    return {'x': x, 'itok_B_6_15': itok_B_6_15, 'L0_cond_base_weight': _L0_cond_in['base_weight'], 'L0_cond_base_bias': _L0_cond_in['base_bias'], 'L0_cond_lora_A_w': _L0_cond_in['lora_A_w'], 'L0_cond_lora_B_w': _L0_cond_in['lora_B_w'], 'L0_ffn_Wq': _L0_ffn_in['Wq'], 'L0_ffn_Wr': _L0_ffn_in['Wr'], 'L0_ffn_aux_keys': _L0_ffn_in['aux_keys'], 'L0_ffn_aux_values': _L0_ffn_in['aux_values'], 'L0_ffn_Wvd': _L0_ffn_in['Wvd'], 'L0_ffn_Wvu': _L0_ffn_in['Wvu'], 'L0_ffn_Wu1': _L0_ffn_in['Wu1'], 'L0_ffn_bu1': _L0_ffn_in['bu1'], 'L0_ffn_Wu2': _L0_ffn_in['Wu2'], 'L0_ffn_bu2': _L0_ffn_in['bu2'], 'L0_ffn_gate_w1': _L0_ffn_in['gate_w1'], 'L0_ffn_gate_bias': _L0_ffn_in['gate_bias'], 'L0_ffn_log_rel': _L0_ffn_in['log_rel']}

def reference(x, itok_B_6_15, L0_cond_base_weight, L0_cond_base_bias, L0_cond_lora_A_w, L0_cond_lora_B_w, L0_ffn_Wq, L0_ffn_Wr, L0_ffn_aux_keys, L0_ffn_aux_values, L0_ffn_Wvd, L0_ffn_Wvu, L0_ffn_Wu1, L0_ffn_bu1, L0_ffn_Wu2, L0_ffn_bu2, L0_ffn_gate_w1, L0_ffn_gate_bias, L0_ffn_log_rel):
    import jax
    import jax.numpy as jnp

    def _L0_cond_ref(x, adapter_ids, base_weight, base_bias, lora_A_w, lora_B_w):
        import jax, jax.numpy as jnp
        import numpy as np
        B, S, D_IN, D_OUT = (4, 1024, 2048, 2048)
        RANK, MAX_LORAS = (16, 32)
        result = jnp.einsum('bsd,od->bso', x, base_weight) + base_bias
        A = lora_A_w[adapter_ids]
        Bw = lora_B_w[adapter_ids]
        h = jnp.einsum('bsd,brd->bsr', x, A)
        lora_out = jnp.einsum('bsr,bor->bso', h, Bw)
        result = result + lora_out
        return result.astype(x.dtype)

    def _L0_ffn_ref(hidden_states, Wq, Wr, aux_keys, aux_values, Wvd, Wvu, Wu1, bu1, Wu2, bu2, gate_w1, gate_bias, log_rel):
        import jax, jax.numpy as jnp
        import numpy as np
        HID, BOT, RDIM, NSLOT, K, VB = (2048, 64, 48, 512, 8, 128)
        TAU_LOW, TAU_HIGH, EARLY_EXIT = (0.5, 2.0, 0.05)

        def _uncertainty(h, Wu1, bu1, Wu2, bu2):
            var = jnp.var(h, axis=-1)
            log_var = jnp.log1p(var)
            norm_var = log_var / (jnp.mean(log_var) + 1e-06)
            learned = (jax.nn.gelu(h @ Wu1.T + bu1) @ Wu2.T + bu2)[..., 0]
            return jnp.clip(norm_var * 0.5 + jax.nn.sigmoid(learned) * 2.5, 0.0, 5.0)
        query = hidden_states @ Wq.T
        rq = query @ Wr.T
        rk = aux_keys @ Wr.T
        router_scores = jnp.einsum('bsr,nr->bsn', rq, rk) / np.sqrt(RDIM) + log_rel
        top_scores, top_idx = jax.lax.top_k(router_scores, K)
        sel_keys = aux_keys[top_idx]
        attn = jnp.einsum('bsd,bskd->bsk', query, sel_keys) / np.sqrt(BOT) + log_rel[top_idx]
        w = jax.nn.softmax(attn, axis=-1)
        sel_vals = aux_values[top_idx]
        aux_out = jnp.einsum('bsk,bskh->bsh', w, sel_vals)
        aux_out = aux_out @ Wvd.T @ Wvu.T
        u = _uncertainty(hidden_states, Wu1, bu1, Wu2, bu2)
        u_norm = jnp.clip((u - TAU_LOW) / (TAU_HIGH - TAU_LOW), 0.0, 1.0)
        gate = jax.nn.sigmoid(gate_w1 * u_norm + gate_bias)
        gate = jnp.where(gate < EARLY_EXIT, 0.0, gate)
        return hidden_states + gate[..., None] * aux_out
    x = x + _L0_ffn_ref(_L0_cond_ref(x, itok_B_6_15, L0_cond_base_weight, L0_cond_base_bias, L0_cond_lora_A_w, L0_cond_lora_B_w), L0_ffn_Wq, L0_ffn_Wr, L0_ffn_aux_keys, L0_ffn_aux_values, L0_ffn_Wvd, L0_ffn_Wvu, L0_ffn_Wu1, L0_ffn_bu1, L0_ffn_Wu2, L0_ffn_bu2, L0_ffn_gate_w1, L0_ffn_gate_bias, L0_ffn_log_rel)
    return x

_drawn_inputs = setup_inputs


def setup_inputs(seed=0):
    import zlib

    import numpy as np

    out = dict(_drawn_inputs(seed))
    spreads = {'L0_ffn_bu1': (0.0, 2.0), 'L0_ffn_log_rel': (0.0, 2.0)}
    factors = {'L0_cond_base_bias': 8.0,
     'L0_ffn_Wq': 45.416,
     'L0_ffn_Wr': 50.331,
     'L0_ffn_aux_keys': 44.678,
     'L0_ffn_aux_values': 44.659,
     'L0_ffn_Wvd': 44.582,
     'L0_ffn_Wvu': 44.754,
     'L0_ffn_Wu1': 64.0,
     'L0_ffn_Wu2': 64.0}
    for name, (base, spread) in spreads.items():
        noise = np.random.default_rng([zlib.crc32(name.encode()), seed]).standard_normal(out[name].shape)
        drawn = base * np.exp(spread * noise) if base else spread * noise
        out[name] = jnp.asarray(drawn.astype(out[name].dtype))
    for name, factor in factors.items():
        out[name] = (out[name] * factor).astype(out[name].dtype)
    return out
```

```python
import concourse.bass as bass
from concourse import mybir
from contextlib import ExitStack


P = 128
D = 2048
KT = D // P
NB = 8
S = 512
TT = S // P
RANK = 16
REP = 3
KL = REP * 2 * RANK
BOT = 64
RDIM = 48
SLOTS = 512
VB = 128
FU = D // 4
FT = FU // P
NTOK = NB * S
WCOL = D + BOT
WHALF = D // 2
NXR = 8
NTILES = NB * KT
SENTINEL = -3.0e38
MASKED = -1.0e30


def bass_adaln_ffn(
    nc: bass.Bass,
    ids: bass.AP,
    x: bass.AP,
    w: bass.AP,
    base_bias: bass.AP,
    lora_a: bass.AP,
    lora_b: bass.AP,
    wr: bass.AP,
    wr_t: bass.AP,
    keys_t: bass.AP,
    values_t: bass.AP,
    wvd_t: bass.AP,
    bu1: bass.AP,
    wu2: bass.AP,
    bu2: bass.AP,
    gate_w1: bass.AP,
    gate_bias: bass.AP,
    log_rel: bass.AP,
    out: bass.AP,
):
    f32 = mybir.dt.float32
    f32r = mybir.dt.float32r
    ALU = mybir.AluOpType
    ACT = mybir.ActivationFunctionType
    AX = mybir.AxisListType

    h_dram = nc.dram_tensor("h_dram", (NB, KT, P, S), f32, kind="Internal").ap()
    r_dram = nc.dram_tensor("r_dram", (NB, KT, P, S), f32, kind="Internal").ap()

    ctx = ExitStack()
    with ctx:
        def sb(name, shape, dt=f32):
            return ctx.enter_context(nc.sbuf_tensor(name, shape, dt))

        def sem(name):
            return ctx.enter_context(nc.semaphore(name))

        def wait(eng, semaphore, value):
            if isinstance(value, int) and value <= 0:
                return
            eng.wait_ge(semaphore, value)

        xh = sb("xh", [P, KT, S], f32r)
        xl = sb("xl", [P, KT, S], f32r)
        xraw = sb("xraw", [P, NXR, S])
        wraw = sb("wraw", [P, 2, WHALF + BOT])
        wsp = sb("wsp", [P, 2, 2 * WCOL], f32r)
        ids_sb = sb("ids_sb", [1, NB], mybir.dt.int32)
        a_raw = sb("a_raw", [P, KT, RANK])
        a_sp = sb("a_sp", [P, KT, REP, 2, RANK], f32r)
        b_raw = sb("b_raw", [KL, S])
        b_sp = sb("b_sp", [KL, TT, S], f32r)
        ax_sp = sb("ax_sp", [KL, S], f32r)
        stage = sb("stage", [P, 4, S])
        h_sp = sb("h_sp", [P, 2, 2, S], f32r)
        sq = sb("sq", [P, S])
        sum_h = sb("sum_h", [P, S])
        sum_hh = sb("sum_hh", [P, S])
        qa = sb("qa", [P, S], f32r)
        qb = sb("qb", [P, S], f32r)
        rep = sb("rep", [P, S])
        att = sb("att", [P, S])
        wt_sp = sb("wt_sp", [P, 2, TT, P], f32r)
        g_a = sb("g_a", [P, SLOTS], f32r)
        g_b = sb("g_b", [P, SLOTS], f32r)
        k_a = sb("k_a", [P, SLOTS], f32r)
        k_b = sb("k_b", [P, SLOTS], f32r)
        v_sp = sb("v_sp", [P, 2, TT, VB], f32r)
        z_all = sb("z_all", [P, NB, S])
        ident = sb("ident", [P, P])
        ones = sb("ones", [P, P])
        bias_sb = sb("bias_sb", [P, KT])
        bu1_sb = sb("bu1_sb", [P, FT])
        wu2_sb = sb("wu2_sb", [P, FT])
        bu2_sb = sb("bu2_sb", [P, 1])
        bu2_half = sb("bu2_half", [P, 1])
        gw_sb = sb("gw_sb", [P, 1])
        gb_sb = sb("gb_sb", [P, 1])
        gb_half = sb("gb_half", [P, 1])
        gw_half = sb("gw_half", [P, 1])
        top8 = sb("top8", [P, 8])
        nmax = sb("nmax", [P, 1])
        esum = sb("esum", [P, 1])
        rsum = sb("rsum", [P, 1])
        stats = sb("stats", [P, NB, 2, TT])
        mean_t = sb("mean_t", [P, NB, TT])
        var_t = sb("var_t", [P, NB, TT])
        norm_t = sb("norm_t", [P, NB, TT])
        rowsum = sb("rowsum", [P, 1])
        inv_t = sb("inv_t", [P, 1])
        sg = sb("sg", [P, TT])
        un = sb("un", [P, TT])
        gt = sb("gt", [P, TT])
        keep = sb("keep", [P, TT])
        carrier = sb("carrier", [P, 1])

        gact = wraw[:].rearrange("p a n -> p (a n)")[:, 0:FT * S].rearrange("p (m s) -> p m s", m=FT)
        acc = sum_h
        diag = sum_hh
        zg = sq
        z_sp = wsp[:, 1, 0:2 * S].rearrange("p (a s) -> p a s", a=2)
        wvu_hi = wsp[:, 0, 0:D]
        wvu_lo = wsp[:, 0, WCOL + BOT:WCOL + BOT + D]
        r_last = [xraw[:, 4 + o, :] for o in range(4)] + [xraw[:, o, :] for o in range(4)] \
            + [z_all[:, b, :] for b in range(NB - 1)] + [rep[:]]
        h_in = xraw[:, 0:4, :]
        r_in = xraw[:, 4:8, :]

        wvd_sb = z_all[:, 4:8, :].rearrange("p b (k v) -> p (b k) v", v=VB)
        values_in = z_all[:, 0:4, :]
        keys_sb = stage[0:BOT, 0, :]
        rk_sb = stage[0:RDIM, 1, :]
        wr_sb = stage[0:RDIM, 2, 0:BOT]
        wrt_sb = stage[0:BOT, 3, 0:RDIM]

        bank = [ctx.enter_context(nc.psum_tensor(f"bank{i}", [P, 512], f32)) for i in range(8)]
        main_ps = bank[0:2]
        q_ps, lora_ps, sc_ps, at_ps, wt_ps, z_ps = bank[2:8]
        stat_ps = z_ps[:, P:P + 2 * TT]
        aux_last = [bank[4], bank[5], bank[0], bank[1]]
        u_ps = [bank[0], bank[1], bank[3], bank[2]]
        aux_ps = bank[4:6]
        gate_ps = bank[6]
        learned_ps = bank[7][:, 0:TT]
        mean_ps = bank[7][:, 8:9]

        ids_in = sem("ids_in")
        keys_in = sem("keys_in")
        small_in = sem("small_in")
        wvd_in = sem("wvd_in")
        values_ready = [sem(f"values_ready{i}") for i in range(4)]
        raw_in = [sem(f"raw_in{i}") for i in range(NXR)]
        w_in = [sem(f"w_in{i}") for i in range(2)]
        a_in = sem("a_in")
        b_in = sem("b_in")
        consts = sem("consts")
        setup_pe = sem("setup_pe")
        setup_act = sem("setup_act")
        setup_dve = sem("setup_dve")
        vslice_used = sem("vslice_used")
        xh_ready = sem("xh_ready")
        xl_ready = sem("xl_ready")
        x_used = sem("x_used")
        wh_ready = sem("wh_ready")
        wl_ready = sem("wl_ready")
        ah_ready = sem("ah_ready")
        al_ready = sem("al_ready")
        bh_ready = sem("bh_ready")
        bl_ready = sem("bl_ready")
        lora_done = sem("lora_done")
        axh_ready = sem("axh_ready")
        ax_ready = sem("ax_ready")
        main_done = sem("main_done")
        h_ready = sem("h_ready")
        sq_ready = sem("sq_ready")
        hh_ready = sem("hh_ready")
        hl_ready = sem("hl_ready")
        h_used = sem("h_used")
        s1_ready = sem("s1_ready")
        s2_ready = sem("s2_ready")
        rx_ready = sem("rx_ready")
        r_ready = sem("r_ready")
        h_out = [sem(f"h_out{i}") for i in range(2)]
        r_out = [sem(f"r_out{i}") for i in range(2)]
        qt_ready = sem("qt_ready")
        qf_ready = sem("qf_ready")
        qh_ready = sem("qh_ready")
        qab_ready = sem("qab_ready")
        stats_done = sem("stats_done")
        stats_ready = sem("stats_ready")
        scores_done = sem("scores_done")
        topk = sem("topk")
        exp_ready = sem("exp_ready")
        rsum_ready = sem("rsum_ready")
        wgt_ready = sem("wgt_ready")
        wt_done = sem("wt_done")
        wth_ready = sem("wth_ready")
        wtl_ready = sem("wtl_ready")
        z_done = sem("z_done")
        z_ready = sem("z_ready")
        mstep = sem("mstep")
        ln_ready = sem("ln_ready")
        mean_done = sem("mean_done")
        u_done = sem("u_done")
        gelu_ready = sem("gelu_ready")
        acc_step = sem("acc_step")
        learned_done = sem("learned_done")
        tanh_ready = sem("tanh_ready")
        gate_step = sem("gate_step")
        gate_done = sem("gate_done")
        zg_ready = sem("zg_ready")
        zgh_ready = sem("zgh_ready")
        zgl_ready = sem("zgl_ready")
        aux_done = sem("aux_done")
        out_ready = sem("out_ready")
        r_tail_in = sem("r_tail_in")
        out_in = [sem(f"out_in{i}") for i in range(4)]

        SUB = ALU.subtract
        TOPK_STEPS = 5
        GATE_STEPS = 9
        LATE_SLICE = 12
        WVU_STEPS = (6, 9)
        QUERY_STEP = [4, 4, 5, 5]
        AUX_AT = {k: [] for k in range(KT)}
        for i in range(KT):
            AUX_AT[6 + i // 2 if i < 14 else i - 1].append(i)
        STEP_OF = {o: k for k, os in AUX_AT.items() for o in os}

        block = ctx.enter_context(nc.Block())

        @block.sync
        def _(sp):
            sp.dma_start(ids_sb[:], ids).then_inc(ids_in, 16)

            def load_x(b, k):
                sp.dma_start(xraw[:, k % NXR, :], x[b, k]).then_inc(raw_in[k % NXR], 16)

            def load_w(tile, half):
                n0, n1 = (0, WHALF) if half == 0 else (WHALF, WCOL)
                sp.dma_start(wraw[:, half, 0:n1 - n0], w[tile, :, n0:n1]).then_inc(w_in[half], 16)

            def adapter(b):
                return sp.value_load(ids_sb[0:1, bass.ds(b, 1)], min_val=0, max_val=lora_a.shape[0] - 1)

            def load_b(b, c):
                which = adapter(b)
                wait(sp, bl_ready, b * TT + c)
                for r in range(2 * REP):
                    sp.dma_start(b_raw[r * RANK:(r + 1) * RANK, :], lora_b[which, c]).then_inc(b_in, 16)

            for k in range(NXR // 2):
                load_x(0, k)
            sp.wait_ge(ids_in, 16)
            sp.dma_start(a_raw[:], lora_a[adapter(0)]).then_inc(a_in, 16)
            for k in range(NXR // 2, NXR):
                load_x(0, k)
            for k in range(NXR, KT):
                sp.wait_ge(xl_ready, k - NXR + 1)
                load_x(0, k)
                if k == NXR + 1:
                    load_w(0, 0)
                if k == NXR + 3:
                    load_w(0, 1)
            load_b(0, 0)
            sp.dma_start(keys_sb, keys_t).then_inc(keys_in, 16)
            sp.dma_start(wr_sb, wr).then_inc(keys_in, 16)
            sp.dma_start(wrt_sb, wr_t).then_inc(keys_in, 16)
            sp.dma_start(rep[BOT:BOT + 1, :], log_rel).then_inc(keys_in, 16)
            sp.dma_start(rep[96:97, :], log_rel).then_inc(keys_in, 16)
            sp.dma_start(bias_sb[:], base_bias).then_inc(small_in, 16)
            sp.dma_start(bu1_sb[:], bu1).then_inc(small_in, 16)
            sp.dma_start(wu2_sb[:], wu2).then_inc(small_in, 16)
            for dst, src in ((bu2_sb, bu2), (gw_sb, gate_w1), (gb_sb, gate_bias)):
                sp.dma_start(dst[:], src.broadcast_to([P, 1])).then_inc(small_in, 16)

            def row(b, last, values=False):
                for o in range(KT):
                    n = b * KT + o
                    if values:
                        if o == 0:
                            sp.dma_start(wvd_sb, wvd_t).then_inc(wvd_in, 16)
                        wait(sp, vslice_used, o - 4 + 1)
                        sp.dma_start(values_in[:, o % 4, :], values_t[o]).then_inc(values_ready[o % 4], 16)
                    tile = (o + 1) % KT if not (last and o == KT - 1) else KT
                    for half in range(2):
                        wait(sp, wl_ready, 2 * n + half + 1)
                        load_w(tile, half)
                    if o == 1 and not last:
                        which = adapter(b + 1)
                        wait(sp, al_ready, b + 1)
                        sp.dma_start(a_raw[:], lora_a[which]).then_inc(a_in, 16)
                    if o % TT == 1 and not (last and o > KT - TT):
                        load_b(b + (o // TT + 1) // TT, (o // TT + 1) % TT)
                    if o == 2:
                        for k in range(NXR):
                            wait(sp, xl_ready, b * KT + k + NXR + 1)
                            load_x(b + 1, k)
                for k in range(NXR, KT):
                    wait(sp, xl_ready, (b + 1) * KT + k - NXR + 1)
                    load_x(b + 1, k)

            row(0, False, values=True)
            row(1, False)
            with sp.Fori(2, NB - 1) as b:
                row(b, False)
            row(NB - 1, True)

            def load_r(c, o):
                if isinstance(c, int) and c == 0 and o < 4:
                    sp.wait_ge(xl_ready, NB * KT + 12 + o + 1)
                else:
                    wait(sp, out_ready, c * KT + o - 4 + 1)
                sp.dma_start(r_in[:, o % 4, :], r_dram[c, o]).then_inc(raw_in[4 + o % 4], 16)

            def load_r_last():
                c = NB - 1
                for o in range(KT):
                    if o < 4:
                        load_r(c, o)
                    elif o < 8:
                        sp.wait_ge(hl_ready, NTILES + c * KT + 12 + o - 4 + 1)
                        sp.dma_start(r_last[o], r_dram[c, o]).then_inc(raw_in[o - 4], 16)
                    else:
                        if o == 8:
                            sp.wait_ge(zg_ready, c)
                        sp.dma_start(r_last[o], r_dram[c, o]).then_inc(r_tail_in, 16)

            def row2(c, h_row, r_row):
                for k in range(KT):
                    if h_row:
                        if isinstance(c, int) and c == 0 and k < 4:
                            sp.wait_ge(xl_ready, NB * KT + 8 + k + 1)
                        else:
                            wait(sp, hl_ready, NTILES + c * KT + k - 4 + 1)
                        sp.dma_start(h_in[:, k % 4, :], h_dram[c, k]).then_inc(raw_in[k % 4], 16)
                    if r_row:
                        for o in range(KT):
                            if (k == 4 if o < 4 else k == min(KT - 1, STEP_OF[o - 4] + 3)):
                                load_r(c - 1, o)

            for i in range(2):
                sp.wait_ge(h_out[i], 16 * KT // 2)
            row2(0, True, False)
            for i in range(2):
                sp.wait_ge(h_out[i], 16 * NTILES // 2)
                sp.wait_ge(r_out[i], 16 * NTILES // 2)
            row2(1, True, True)
            with sp.Fori(2, NB) as c:
                row2(c, True, True)
            load_r_last()
            for i in range(4):
                sp.wait_ge(out_in[i], 16 * NB * KT // 4)

        @block.gpsimd
        def _(pool):
            filled = ((ones[:], 1.0), (ident[:], 0.0), (qb[BOT:P, :].bitcast(f32), 1.0),
                      (g_b[BOT:P, :].bitcast(f32), 0.0), (k_b[BOT:P, :].bitcast(f32), 0.0))
            for i, (tile, value) in enumerate(filled):
                wait(pool, consts, i)
                pool.memset(tile, value).then_inc(consts, 1)
            pool.wait_ge(consts, 5)
            pool.affine_select(out=ident[:], in_=ident[:], compare_op=ALU.not_equal, fill=1.0, base=0,
                               pattern=[[-1, P]], channel_multiplier=1).then_inc(consts, 1)

        @block.scalar
        def _(act):
            def to_hi(dst, src):
                return act.activation(dst, src, ACT.Copy)

            def split_x_hi(b, k):
                wait(act, raw_in[k % NXR], 16 * (2 * b + k // NXR + 1))
                wait(act, x_used, (b - 1) * KT + k + 1)
                wait(act, r_ready, (b - 1) * KT + k + 1)
                to_hi(xh[:, k, :], xraw[:, k % NXR, :]).then_inc(xh_ready, 1)

            def split_w_hi(m, slot, halves):
                for half in halves:
                    n = WHALF + half * BOT
                    wait(act, w_in[half], 16 * (m + 1))
                    if half == 0:
                        wait(act, h_used, m - 1)
                    to_hi(wsp[:, slot, half * WHALF:half * WHALF + n], wraw[:, half, 0:n])\
                        .then_inc(wh_ready, 1)

            def split_a_hi(b):
                wait(act, a_in, 16 * (b + 1))
                wait(act, lora_done, b)
                for r in range(REP):
                    last = to_hi(a_sp[:, :, r, 0, :], a_raw[:])
                last.then_inc(ah_ready, 1)

            def exp_tile(i):
                wait(act, topk, TOPK_STEPS * (i + 1))
                act.activation(att[:], att[:], ACT.Exp, bias=nmax[:], accum_out=esum[:])\
                    .then_inc(exp_ready, 1)

            def wt_hi(i):
                wait(act, wt_done, i + 1)
                wait(act, z_done, i)
                to_hi(wt_sp[:, 0, :, :], wt_ps[:].rearrange("p (s t) -> p s t", s=TT))\
                    .then_inc(wth_ready, 1)

            def z_copy(b, t):
                wait(act, z_done, b * TT + t + 1)
                act.activation(z_all[:, b, t * P:(t + 1) * P], z_ps[:, 0:P], ACT.Copy)\
                    .then_inc(z_ready, 1)

            def query_hi(b):
                wait(act, h_used, (b + 1) * KT)
                wait(act, wgt_ready, b * TT)
                wait(act, wt_done, b * TT)
                act.activation(att[0:BOT, :], q_ps[BOT:P, :], ACT.Copy).then_inc(qt_ready, 1)
                wait(act, qf_ready, b + 1)
                wait(act, scores_done, b * TT)
                act.activation(qa[0:BOT, :], rep[0:BOT, :], ACT.Copy).then_inc(qh_ready, 1)
                act.activation(qb[0:BOT, :], rep[0:BOT, :], ACT.Copy).then_inc(qh_ready, 1)

            def router_key_product():
                act.wait_ge(setup_pe, 1)
                act.activation(rk_sb, main_ps[1][0:RDIM, :], ACT.Copy).then_inc(setup_act, 1)

            def factors_hi():
                act.wait_ge(keys_in, 80)
                act.wait_ge(setup_pe, 2)
                act.activation(att[0:BOT, :], q_ps[0:BOT, :], ACT.Copy, scale=float(RDIM) ** -0.5)
                act.activation(sq[0:BOT, :], keys_sb, ACT.Copy, scale=float(BOT) ** -0.5)\
                    .then_inc(setup_act, 1)
                act.wait_ge(setup_act, 2)
                act.wait_ge(consts, 6)
                for dst_a, dst_b, src in ((g_a, g_b, att), (k_a, k_b, sq)):
                    to_hi(dst_a[0:BOT, :], src[0:BOT, :])
                    to_hi(dst_a[BOT:P, :], src[0:BOT, :])
                    to_hi(dst_b[BOT:BOT + 1, :], rep[BOT:BOT + 1, :])
                    to_hi(dst_b[96:97, :], rep[96:97, :]).then_inc(setup_act, 1)
                act.wait_ge(small_in, 96)
                act.activation(gb_half[:], gb_sb[:], ACT.Copy, scale=0.5)
                act.activation(gw_half[:], gw_sb[:], ACT.Copy, scale=0.5)
                act.activation(bu2_half[:], bu2_sb[:], ACT.Copy, scale=0.5)

            def values_hi():
                act.wait_ge(vslice_used, KT)
                for s in range(TT):
                    last = to_hi(v_sp[:, 0, s, :], bank[4 + s][:, 0:VB])
                last.then_inc(setup_act, 1)

            act.wait_ge(consts, 1)
            act.activation(nmax[:], ones[:, 0:1], ACT.Copy)
            for k in range(KT):
                split_x_hi(0, k)
                if k == 2:
                    split_a_hi(0)
            split_w_hi(0, 0, (0, 1))
            router_key_product()

            def store_h(b, o):
                act.dma_start(h_dram[b, o], stage[:, o % 2, :]).then_inc(h_out[o % 2], 16)

            def store_r(b, o):
                wait(act, r_ready, b * KT + o + 1)
                act.dma_start(r_dram[b, o], stage[:, 2 + o % 2, :]).then_inc(r_out[o % 2], 16)

            def row(b, first, last):
                wait(act, lora_done, b + 1)
                wait(act, main_done, b * KT)
                to_hi(ax_sp[:], lora_ps[0:KL, :]).then_inc(axh_ready, 1)
                for o in range(KT):
                    n = b * KT + o
                    t = o // TT
                    if not first and o % TT == 3:
                        wt_hi((b - 1) * TT + t)
                    if o == KT - 1:
                        for k in range(LATE_SLICE if last else KT - 1):
                            split_x_hi(b + 1, k)
                    if o % TT == 0:
                        wait(act, b_in, 2 * REP * 16 * (b * TT + t + 1))
                        wait(act, main_done, b * KT)
                        to_hi(b_sp[:, t, :], b_raw[:]).then_inc(bh_ready, 1)
                    if o < KT - 1:
                        split_w_hi(n + 1, (o + 1) % 2, (0, 1))
                    if o == 0 and not first:
                        query_hi(b - 1)
                    if not first and o % TT == 1:
                        exp_tile((b - 1) * TT + t)
                    if o == 2 and not last:
                        split_a_hi(b + 1)
                    if first and o == 0:
                        factors_hi()
                    slot = o % 2
                    wait(act, main_done, n + 1)
                    wait(act, hl_ready, n - 1)
                    wait(act, h_out[slot], 16 * (b * (KT // 2) + o // 2))
                    act.activation(stage[:, slot, :], main_ps[slot][:], ACT.Identity,
                                   bias=bias_sb[:, o:o + 1]).then_inc(h_ready, 1)
                    wait(act, h_used, n - 1)
                    wait(act, h_ready, n + 1)
                    to_hi(h_sp[:, slot, 0, :], stage[:, slot, :]).then_inc(hh_ready, 1)
                    if o == KT - 1 and not last:
                        split_w_hi(n + 1, 0, (0,))
                        split_x_hi(b + 1, KT - 1)
                        split_w_hi(n + 1, 0, (1,))
                    wait(act, s2_ready, n)
                    if first and o == 0:
                        act.wait_ge(setup_dve, 2)
                    act.activation(sq[:], stage[:, slot, :], ACT.Square).then_inc(sq_ready, 1)
                    store_h(b, o)
                    if o > 0:
                        store_r(b, o - 1)
                    if not first and o % TT == 3:
                        z_copy(b - 1, t)
                store_r(b, KT - 1)

            row(0, True, False)
            values_hi()
            row(1, False, False)
            with act.Fori(2, NB - 1) as b:
                row(b, False, False)
            row(NB - 1, False, True)

            def h_hi(c, k):
                m = c * KT + k
                wait(act, raw_in[k % 4], 16 * (2 * (NB + 1) + c * (KT // 4) + k // 4 + 1))
                wait(act, h_used, NTILES + m - 1)
                to_hi(h_sp[:, k % 2, 0, :], h_in[:, k % 4, :]).then_inc(hh_ready, 1)

            def gelus(c):
                wait(act, acc_step, c * FT)
                for m in range(FT):
                    if m < FT - 1:
                        wait(act, u_done, (FT - 1) * c + m + 1)
                    else:
                        wait(act, h_used, NTILES + (c + 1) * KT)
                    act.activation(gact[:, m, :], u_ps[m][:], ACT.Gelu_apprx_tanh,
                                   bias=bu1_sb[:, m:m + 1]).then_inc(gelu_ready, 1)

            def store_out(c, o):
                wait(act, out_ready, c * KT + o + 1)
                act.dma_start(out[c, o], stage[:, o % 4, :]).then_inc(out_in[o % 4], 16)

            def gate_act(c, k):
                if k == 2:
                    wait(act, learned_done, c + 1)
                    wait(act, gate_step, GATE_STEPS * c)
                    act.activation(sg[:], learned_ps, ACT.Tanh, bias=bu2_half[:], scale=0.5)\
                        .then_inc(tanh_ready, 1)
                if k == 3:
                    wait(act, gate_step, GATE_STEPS * c + 5)
                    act.activation(gt[:], un[:], ACT.Tanh, bias=gb_half[:], scale=gw_half[:])\
                        .then_inc(tanh_ready, 1)
                if k == 5:
                    wait(act, zg_ready, c + 1)
                    wait(act, aux_done, c * KT)
                    to_hi(z_sp[:, 0, :], zg[:]).then_inc(zgh_ready, 1)

            def row2(c, u_row, aux_row, first=False):
                for k in range(KT):
                    if u_row:
                        h_hi(c, k)
                    if first:
                        if k == 0:
                            query_hi(NB - 1)
                        if k < KT - LATE_SLICE:
                            split_x_hi(NB, LATE_SLICE + k)
                        if k in WVU_STEPS:
                            split_w_hi(NTILES, 0, (WVU_STEPS.index(k),))
                        if k % 3 == 1 and k > 1:
                            wt_hi((NB - 1) * TT + k // 3 - 1)
                        if k % 3 == 2 and k > 2:
                            z_copy(NB - 1, k // 3 - 1)
                        if k % 3 == 2 and k < 12:
                            exp_tile((NB - 1) * TT + k // 3)
                        if k == 14:
                            wait(act, mstep, 4)
                            act.activation(norm_t[:], var_t[:], ACT.Ln, bias=1.0).then_inc(ln_ready, 1)
                    if aux_row:
                        if k == 0:
                            gelus(c - 1)
                        gate_act(c - 1, k)
                        for o in AUX_AT[k]:
                            if o > 0:
                                store_out(c - 1, o - 1)
                if aux_row:
                    store_out(c - 1, KT - 1)

            row2(0, True, False, first=True)
            row2(1, True, True)
            with act.Fori(2, NB) as c:
                row2(c, True, True)
            row2(NB, False, True)

        @block.vector
        def _(dve):
            def lo(dst, src, hi):
                return dve.tensor_tensor(dst, src, hi.bitcast(f32), SUB)

            def split_x_lo(b, k):
                wait(dve, xh_ready, b * KT + k + 1)
                lo(xl[:, k, :], xraw[:, k % NXR, :], xh[:, k, :]).then_inc(xl_ready, 1)

            def split_w_lo(m, slot, halves=(0, 1)):
                if 0 in halves:
                    wait(dve, wh_ready, 2 * m + 1)
                    lo(wsp[:, slot, WCOL + BOT:WCOL + BOT + WHALF], wraw[:, 0, 0:WHALF],
                       wsp[:, slot, 0:WHALF]).then_inc(wl_ready, 1)
                if 1 in halves:
                    wait(dve, wh_ready, 2 * m + 2)
                    lo(wsp[:, slot, WCOL:WCOL + BOT], wraw[:, 1, WHALF:WHALF + BOT], wsp[:, slot, D:WCOL])
                    lo(wsp[:, slot, WCOL + BOT + WHALF:2 * WCOL], wraw[:, 1, 0:WHALF],
                       wsp[:, slot, WHALF:D]).then_inc(wl_ready, 1)

            def split_a_lo(b):
                wait(dve, ah_ready, b + 1)
                for r in range(REP):
                    last = lo(a_sp[:, :, r, 1, :], a_raw[:], a_sp[:, :, r, 0, :])
                last.then_inc(al_ready, 1)

            def carry():
                dve.memset(carrier[:], 0.0)

            def top_eight(i):
                selected(i)
                masked(i)

            def selected(i):
                wait(dve, scores_done, i + 1)
                carry()
                dve.max(top8[:], sc_ps[:]).then_inc(topk, 1)
                wait(dve, topk, TOPK_STEPS * i + 1)
                carry()
                dve.match_replace(rep[:], top8[:], sc_ps[:], SENTINEL).then_inc(topk, 1)

            def masked(i):
                wait(dve, topk, TOPK_STEPS * i + 2)
                dve.tensor_scalar(rep[:], rep[:], SENTINEL, MASKED, ALU.not_equal, ALU.mult)\
                    .then_inc(topk, 1)
                wait(dve, topk, TOPK_STEPS * i + 3)
                wait(dve, wt_done, i)
                dve.tensor_tensor(att[:], at_ps[:], rep[:], ALU.add).then_inc(topk, 1)
                wait(dve, topk, TOPK_STEPS * i + 4)
                dve.tensor_reduce(nmax[:], att[:], AX.X, ALU.max, negate=True).then_inc(topk, 1)

            def normalise(i):
                wait(dve, exp_ready, i + 1)
                dve.reciprocal(rsum[:], esum[:]).then_inc(rsum_ready, 1)
                wait(dve, rsum_ready, i + 1)
                dve.tensor_scalar(att[:], att[:], rsum[:], None, ALU.mult).then_inc(wgt_ready, 1)

            def wt_lo(i):
                wait(dve, wth_ready, i + 1)
                lo(wt_sp[:, 1, :, :], wt_ps[:].rearrange("p (s t) -> p s t", s=TT), wt_sp[:, 0, :, :])\
                    .then_inc(wtl_ready, 1)

            def query_lo(b):
                wait(dve, qt_ready, b + 1)
                dve.tensor_tensor(rep[0:BOT, :], q_ps[0:BOT, :], att[0:BOT, :], ALU.add)\
                    .then_inc(qf_ready, 1)
                wait(dve, qh_ready, 2 * b + 1)
                wait(dve, qf_ready, b + 1)
                lo(qa[BOT:P, :], rep[0:BOT, :], qa[0:BOT, :]).then_inc(qab_ready, 1)

            def copy_stats(b):
                wait(dve, stats_done, b + 1)
                dve.tensor_copy(stats[:, b, :, :], stat_ps.rearrange("p (a t) -> p a t", a=2))\
                    .then_inc(stats_ready, 1)

            def factors_lo():
                dve.wait_ge(setup_act, 3)
                lo(g_b[0:BOT, :], att[0:BOT, :], g_a[0:BOT, :])
                lo(g_b[96:97, :], rep[96:97, :], g_b[96:97, :]).then_inc(setup_dve, 1)
                dve.wait_ge(setup_act, 4)
                lo(k_b[0:BOT, :], sq[0:BOT, :], k_a[0:BOT, :])
                lo(k_b[96:97, :], rep[96:97, :], k_b[96:97, :]).then_inc(setup_dve, 1)

            def values_lo():
                dve.wait_ge(setup_act, 5)
                for s in range(TT):
                    last = lo(v_sp[:, 1, s, :], bank[4 + s][:, 0:VB], v_sp[:, 0, s, :])
                last.then_inc(setup_dve, 1)

            for k in range(KT):
                split_x_lo(0, k)
                if k == 2:
                    split_a_lo(0)
            split_w_lo(0, 0)

            def row(b, first, last):
                wait(dve, axh_ready, b + 1)
                lo(ax_sp[2 * RANK:4 * RANK, :], lora_ps[2 * RANK:4 * RANK, :],
                   ax_sp[2 * RANK:4 * RANK, :]).then_inc(ax_ready, 1)
                for o in range(KT):
                    n = b * KT + o
                    t = o // TT
                    slot = o % 2
                    if not first and o % TT == 1:
                        top_eight((b - 1) * TT + t)
                    if not first and o % TT == 3:
                        wt_lo((b - 1) * TT + t)
                    if o == KT - 1:
                        for k in range(LATE_SLICE if last else KT - 1):
                            split_x_lo(b + 1, k)
                    if o % TT == 0:
                        wait(dve, bh_ready, b * TT + t + 1)
                        lo(b_sp[4 * RANK:KL, t, :], b_raw[4 * RANK:KL, :], b_sp[4 * RANK:KL, t, :])\
                            .then_inc(bl_ready, 1)
                    if o < KT - 1:
                        split_w_lo(n + 1, (o + 1) % 2)
                    if o == 0 and not first:
                        copy_stats(b - 1)
                        query_lo(b - 1)
                    if not first and o % TT == 1:
                        normalise((b - 1) * TT + t)
                    if o == 2 and not last:
                        split_a_lo(b + 1)
                    if first and o == 0:
                        factors_lo()
                    h_tile = stage[:, slot, :]
                    r_tile = stage[:, 2 + slot, :]
                    wait(dve, h_ready, n + 1)
                    wait(dve, r_out[slot], 16 * (b * (KT // 2) + o // 2))
                    dve.tensor_tensor(r_tile, h_tile, xl[:, o, :].bitcast(f32), ALU.add)\
                        .then_inc(rx_ready, 1)
                    wait(dve, rx_ready, n + 1)
                    dve.tensor_tensor(r_tile, r_tile, xh[:, o, :].bitcast(f32), ALU.add)\
                        .then_inc(r_ready, 1)
                    if o == KT - 1 and not last:
                        split_w_lo(n + 1, 0, (0,))
                        split_x_lo(b + 1, KT - 1)
                    if o == 0:
                        wait(dve, stats_done, b)
                        dve.tensor_copy(sum_h[:], h_tile).then_inc(s1_ready, 1)
                    else:
                        wait(dve, s1_ready, n)
                        dve.tensor_tensor(sum_h[:], sum_h[:], h_tile, ALU.add).then_inc(s1_ready, 1)
                    wait(dve, hh_ready, n + 1)
                    lo(h_sp[:, slot, 1, :], h_tile, h_sp[:, slot, 0, :]).then_inc(hl_ready, 1)
                    if o == KT - 1 and not last:
                        split_w_lo(n + 1, 0, (1,))
                    wait(dve, sq_ready, n + 1)
                    if o == 0:
                        dve.tensor_copy(sum_hh[:], sq[:]).then_inc(s2_ready, 1)
                    else:
                        wait(dve, s2_ready, n)
                        dve.tensor_tensor(sum_hh[:], sum_hh[:], sq[:], ALU.add).then_inc(s2_ready, 1)

            row(0, True, False)
            values_lo()
            row(1, False, False)
            with dve.Fori(2, NB - 1) as b:
                row(b, False, False)
            row(NB - 1, False, True)

            def variances():
                dve.wait_ge(stats_ready, NB)
                dve.tensor_scalar(mean_t[:], stats[:, :, 0, :], 1.0 / D, None, ALU.mult).then_inc(mstep, 1)
                dve.wait_ge(mstep, 1)
                dve.tensor_tensor(mean_t[:], mean_t[:], mean_t[:], ALU.mult).then_inc(mstep, 1)
                dve.wait_ge(mstep, 2)
                dve.scalar_tensor_tensor(var_t[:], stats[:, :, 1, :], 1.0 / D, mean_t[:], ALU.mult, SUB)\
                    .then_inc(mstep, 1)
                dve.wait_ge(mstep, 3)
                dve.tensor_scalar(var_t[:], var_t[:], 0.0, None, ALU.max).then_inc(mstep, 1)

            def mean_of_logs():
                dve.wait_ge(ln_ready, 1)
                dve.tensor_reduce(rowsum[:], norm_t[:].rearrange("p b t -> p (b t)"), AX.X, ALU.add)\
                    .then_inc(mstep, 1)
                dve.wait_ge(mean_done, 1)
                dve.tensor_scalar(inv_t[:], mean_ps, 1.0 / NTOK, 1e-6, ALU.mult, ALU.add).then_inc(mstep, 1)
                dve.wait_ge(mstep, 6)
                dve.reciprocal(inv_t[:], inv_t[:]).then_inc(mstep, 1)
                dve.wait_ge(mstep, 7)
                dve.tensor_scalar(norm_t[:], norm_t[:], inv_t[:], 0.5, ALU.mult, ALU.mult).then_inc(mstep, 1)

            def gate_dve(c, k):
                step = GATE_STEPS * c
                if k < 2:
                    if k == 0:
                        wait(dve, learned_done, c)
                    for m in range(k * FT // 2, (k + 1) * FT // 2):
                        wait(dve, gelu_ready, c * FT + m + 1)
                        if m == 0:
                            dve.tensor_scalar(acc[:], gact[:, 0, :], wu2_sb[:, 0:1], None, ALU.mult)\
                                .then_inc(acc_step, 1)
                        else:
                            wait(dve, acc_step, c * FT + m)
                            dve.scalar_tensor_tensor(acc[:], gact[:, m, :], wu2_sb[:, m:m + 1], acc[:],
                                                     ALU.mult, ALU.add).then_inc(acc_step, 1)
                if k == 2:
                    wait(dve, tanh_ready, 2 * c + 1)
                    dve.tensor_scalar(un[:], sg[:], 1.25, 1.25, ALU.mult, ALU.add).then_inc(gate_step, 1)
                    wait(dve, gate_step, step + 1)
                    dve.tensor_tensor(un[:], un[:], norm_t[:, c, :], ALU.add).then_inc(gate_step, 1)
                    wait(dve, gate_step, step + 2)
                    dve.tensor_scalar(un[:], un[:], 0.0, 5.0, ALU.max, ALU.min).then_inc(gate_step, 1)
                    wait(dve, gate_step, step + 3)
                    dve.tensor_scalar(un[:], un[:], 0.5, 1.0 / 1.5, SUB, ALU.mult).then_inc(gate_step, 1)
                    wait(dve, gate_step, step + 4)
                    dve.tensor_scalar(un[:], un[:], 0.0, 1.0, ALU.max, ALU.min).then_inc(gate_step, 1)
                if k == 3:
                    wait(dve, tanh_ready, 2 * c + 2)
                    dve.tensor_scalar(gt[:], gt[:], 0.5, 0.5, ALU.mult, ALU.add).then_inc(gate_step, 1)
                    wait(dve, gate_step, step + 6)
                    dve.tensor_scalar(keep[:], gt[:], 0.05, None, ALU.is_ge).then_inc(gate_step, 1)
                    wait(dve, gate_step, step + 7)
                    dve.tensor_tensor(gt[:], gt[:], keep[:], ALU.mult).then_inc(gate_step, 1)
                    wait(dve, gate_step, step + 8)
                    wait(dve, gate_done, c)
                    for t in range(TT):
                        last = dve.tensor_scalar(diag[:, t * P:(t + 1) * P], ident[:], gt[:, t:t + 1], None,
                                                 ALU.mult)
                    last.then_inc(gate_step, 1)
                if k == 4:
                    wait(dve, gate_done, c + 1)
                    wait(dve, zgl_ready, c)
                    dve.tensor_tensor(zg[:], gate_ps[:], z_all[:, c, :], ALU.mult).then_inc(zg_ready, 1)
                if k == 5:
                    wait(dve, zgh_ready, c + 1)
                    lo(z_sp[:, 1, :], zg[:], z_sp[:, 0, :]).then_inc(zgl_ready, 1)

            def add_out_last(o):
                c = NB - 1
                wait(dve, aux_done, c * KT + o + 1)
                if o < 8:
                    rows = c * (KT // 4) if o < 4 else NB * (KT // 4)
                    wait(dve, raw_in[(4 + o) % 8], 16 * (2 * (NB + 1) + rows + 1))
                elif o == 8:
                    dve.wait_ge(r_tail_in, 16 * 8)
                wait(dve, out_in[o % 4], 16 * (c * (KT // 4) + o // 4))
                dve.tensor_tensor(stage[:, o % 4, :], aux_last[o % 4][:], r_last[o], ALU.add)\
                    .then_inc(out_ready, 1)

            def add_out(c, o):
                wait(dve, aux_done, c * KT + o + 1)
                wait(dve, raw_in[4 + o % 4], 16 * (2 * (NB + 1) + c * (KT // 4) + o // 4 + 1))
                wait(dve, out_in[o % 4], 16 * (c * (KT // 4) + o // 4))
                dve.tensor_tensor(stage[:, o % 4, :], aux_ps[o % 2][:], r_in[:, o % 4, :], ALU.add)\
                    .then_inc(out_ready, 1)

            def row2(c, u_row, aux_row, first=False):
                for k in range(KT):
                    if u_row:
                        m = NTILES + c * KT + k
                        wait(dve, hh_ready, m + 1)
                        lo(h_sp[:, k % 2, 1, :], h_in[:, k % 4, :], h_sp[:, k % 2, 0, :])\
                            .then_inc(hl_ready, 1)
                    if first:
                        if k == 0:
                            copy_stats(NB - 1)
                            query_lo(NB - 1)
                        if k < KT - LATE_SLICE:
                            split_x_lo(NB, LATE_SLICE + k)
                        if k == 3:
                            variances()
                        if k in WVU_STEPS:
                            split_w_lo(NTILES, 0, (WVU_STEPS.index(k),))
                        if k % 3 == 1 and k > 1:
                            wt_lo((NB - 1) * TT + k // 3 - 1)
                        if k % 3 == 1 and k < 12:
                            selected((NB - 1) * TT + k // 3)
                        if k % 3 == 2 and k < 12:
                            masked((NB - 1) * TT + k // 3)
                        if k % 3 == 0 and k > 0 and k < 13:
                            normalise((NB - 1) * TT + k // 3 - 1)
                        if k == 15:
                            mean_of_logs()
                            for i in range(2):
                                dve.wait_ge(h_out[i], 16 * NTILES // 2)
                                dve.wait_ge(r_out[i], 16 * NTILES // 2)
                    if aux_row:
                        gate_dve(c - 1, k)
                        for o in AUX_AT[k]:
                            if u_row:
                                add_out(c - 1, o)
                            else:
                                add_out_last(o)

            row2(0, True, False, first=True)
            row2(1, True, True)
            with dve.Fori(2, NB) as c:
                row2(c, True, True)
            row2(NB, False, True)

        @block.tensor
        def _(pe):
            def router_keys():
                pe.wait_ge(keys_in, 80)
                pe.matmul(main_ps[1][0:RDIM, :], wrt_sb, keys_sb, start=True, stop=True)\
                    .then_inc(setup_pe, 1)

            def router_factor():
                pe.wait_ge(setup_act, 1)
                pe.matmul(q_ps[0:BOT, :], wr_sb, rk_sb, start=True, stop=True).then_inc(setup_pe, 1)

            def values_pass(k):
                if k == 0:
                    pe.wait_ge(wvd_in, 16)
                pe.wait_ge(values_ready[k % 4], 16 * (k // 4 + 1))
                for s in range(TT):
                    last = pe.matmul(bank[4 + s][:, 0:VB], values_in[:, k % 4, s * P:(s + 1) * P],
                                     wvd_sb[:, k, :], start=(k == 0), stop=(k == KT - 1))
                last.then_inc(vslice_used, 1)

            def lora_a_pass(b):
                wait(pe, al_ready, b + 1)
                wait(pe, ax_ready, b)
                for k in range(KT):
                    wait(pe, xl_ready, b * KT + k + 1)
                    a_k = a_sp[:, k, :, :, :].rearrange("p r a n -> p (r a n)")
                    pe.matmul(lora_ps[0:KL, :], a_k, xh[:, k, :], start=(k == 0), stop=False)
                    last = pe.matmul(lora_ps[0:KL, :], a_k, xl[:, k, :], start=False, stop=(k == KT - 1))
                last.then_inc(lora_done, 1)

            def query_pass(n, o):
                slot = o % 2
                wait(pe, hl_ready, n + 1)
                wq = wsp[:, slot, D:D + 2 * BOT]
                pe.matmul(q_ps[:], wq, h_sp[:, slot, 0, :], start=(o == 0), stop=False)
                pe.matmul(q_ps[:], wq, h_sp[:, slot, 1, :], start=False, stop=(o == KT - 1)).then_inc(h_used, 1)

            def stats_pass(b):
                wait(pe, s2_ready, (b + 1) * KT)
                wait(pe, z_ready, b * TT)
                for i, s in enumerate((sum_h, sum_hh)):
                    for t in range(TT):
                        last = pe.matmul(stat_ps[:, i * TT + t:i * TT + t + 1], s[:, t * P:(t + 1) * P],
                                         ones[:, 0:1], start=True, stop=True)
                last.then_inc(stats_done, 1)

            def scores(b, t):
                i = b * TT + t
                if t == 0:
                    wait(pe, qab_ready, b + 1)
                    wait(pe, qh_ready, 2 * b + 2)
                wait(pe, topk, TOPK_STEPS * i)
                tok = slice(t * P, (t + 1) * P)
                pe.matmul(sc_ps[:], qa[:, tok], g_a[:], start=True, stop=False)
                pe.matmul(sc_ps[:], qb[:, tok], g_b[:], start=False, stop=True)
                pe.matmul(at_ps[:], qa[:, tok], k_a[:], start=True, stop=False)
                pe.matmul(at_ps[:], qb[:, tok], k_b[:], start=False, stop=True).then_inc(scores_done, 1)

            def transposes(i):
                wait(pe, wgt_ready, i + 1)
                wait(pe, wtl_ready, i)
                for s in range(TT):
                    last = pe.transpose(wt_ps[:, s * P:(s + 1) * P], att[:, s * P:(s + 1) * P], ident[:])
                last.then_inc(wt_done, 1)

            def z_pass(b, t):
                i = b * TT + t
                wait(pe, wtl_ready, i + 1)
                wait(pe, z_ready, i)
                if t == 0:
                    wait(pe, stats_ready, b + 1)
                parts = [(0, 0), (0, 1), (1, 0)]
                for s in range(TT):
                    for j, (v, m) in enumerate(parts):
                        last = pe.matmul(z_ps[:, 0:P], v_sp[:, v, s, :], wt_sp[:, m, s, :],
                                         start=(s == 0 and j == 0), stop=(s == TT - 1 and j == 2))
                last.then_inc(z_done, 1)

            lora_a_pass(0)
            router_keys()

            def row(b, first, last):
                for o in range(KT):
                    n = b * KT + o
                    t = o // TT
                    slot = o % 2
                    acc_ps = main_ps[slot][:]
                    if not first and o % TT == 1:
                        scores(b - 1, t)
                    if not first and o % TT == 3:
                        transposes((b - 1) * TT + t)
                    wait(pe, h_ready, n - 1)
                    for k in range(KT):
                        if k % (KT // 2) == 0:
                            wait(pe, wl_ready, 2 * n + k // (KT // 2) + 1)
                        w_hi = wsp[:, slot, k * P:(k + 1) * P]
                        w_lo = wsp[:, slot, WCOL + BOT + k * P:WCOL + BOT + (k + 1) * P]
                        pe.matmul(acc_ps, w_hi, xh[:, k, :], start=(k == 0), stop=False)
                        pe.matmul(acc_ps, w_hi, xl[:, k, :], start=False, stop=False)
                        last_k = pe.matmul(acc_ps, w_lo, xh[:, k, :], start=False, stop=False)
                        if o == KT - 1:
                            last_k.then_inc(x_used, 1)
                        if first and o == 0 and k == 8:
                            router_factor()
                        if k == QUERY_STEP[o % TT] and not (first and o == 0):
                            if o == 1:
                                wait(pe, qf_ready, b)
                                if first:
                                    pe.wait_ge(setup_act, 2)
                            query_pass(n - 1, (o - 1) % KT)
                            if o == 0:
                                stats_pass(b - 1)
                    if o == 0:
                        wait(pe, ax_ready, b + 1)
                    if o % TT == 0:
                        wait(pe, bl_ready, b * TT + t + 1)
                    pe.matmul(acc_ps, b_sp[:, t, (o % TT) * P:(o % TT + 1) * P], ax_sp[:],
                              start=False, stop=True).then_inc(main_done, 1)
                    if first:
                        values_pass(o)
                    if not first and o % TT == 3:
                        z_pass(b - 1, t)
                if not last:
                    lora_a_pass(b + 1)
                if first:
                    pe.wait_ge(setup_dve, 3)

            row(0, True, False)
            row(1, False, False)
            with pe.Fori(2, NB - 1) as b:
                row(b, False, False)
            row(NB - 1, False, True)

            def u1_pass(c, k):
                m0 = NTILES + c * KT + k
                slot = k % 2
                wait(pe, hl_ready, m0 + 1)
                if isinstance(c, int) and c == 0:
                    pe.wait_ge(xl_ready, NB * KT + k + 1)
                for m in range(FT):
                    if k == 0:
                        if isinstance(c, int) and c == 0:
                            if m == 0:
                                pe.wait_ge(h_ready, NTILES)
                            if m == 3:
                                pe.wait_ge(qf_ready, NB)
                        else:
                            wait(pe, gelu_ready, (c - 1) * FT + m + 1)
                    f = slice(m * P, (m + 1) * P)
                    pe.matmul(u_ps[m][:], xh[:, k, f], h_sp[:, slot, 0, :], start=(k == 0), stop=False)
                    pe.matmul(u_ps[m][:], xh[:, k, f], h_sp[:, slot, 1, :], start=False, stop=False)
                    last = pe.matmul(u_ps[m][:], xl[:, k, f], h_sp[:, slot, 0, :], start=False,
                                     stop=(k == KT - 1))
                    if k == KT - 1 and m < FT - 1:
                        last.then_inc(u_done, 1)
                last.then_inc(h_used, 1)

            def learned_pass(c):
                wait(pe, acc_step, (c + 1) * FT)
                wait(pe, tanh_ready, 2 * c)
                for t in range(TT):
                    last = pe.matmul(learned_ps[:, t:t + 1], acc[:, t * P:(t + 1) * P], ones[:, 0:1],
                                     start=True, stop=True)
                last.then_inc(learned_done, 1)

            def gate_pass(c):
                wait(pe, gate_step, GATE_STEPS * (c + 1))
                wait(pe, zg_ready, c)
                pe.matmul(gate_ps[:], ones[:], diag[:], start=True, stop=True).then_inc(gate_done, 1)

            def aux_pass(c, o, banks):
                if o == 0:
                    wait(pe, zgl_ready, c + 1)
                if banks is aux_ps or o < 2:
                    wait(pe, out_ready, c * KT + o - 1)
                elif o >= 4:
                    wait(pe, out_ready, c * KT + o - 3)
                ps = banks[o % len(banks)][:]
                f = slice(o * P, (o + 1) * P)
                pe.matmul(ps, wvu_hi[:, f], z_sp[:, 0, :], start=True, stop=False)
                pe.matmul(ps, wvu_hi[:, f], z_sp[:, 1, :], start=False, stop=False)
                pe.matmul(ps, wvu_lo[:, f], z_sp[:, 0, :], start=False, stop=True).then_inc(aux_done, 1)

            def row2(c, u_row, aux_row, first=False):
                for k in range(KT):
                    if first and k == 0:
                        query_pass(NTILES - 1, KT - 1)
                        stats_pass(NB - 1)
                    if first and k % 3 == 1 and k > 1:
                        transposes((NB - 1) * TT + k // 3 - 1)
                    if first and k % 3 == 1 and k < 12:
                        scores(NB - 1, k // 3)
                    if aux_row:
                        if k == 2:
                            learned_pass(c - 1)
                        if k == 4:
                            gate_pass(c - 1)
                        for o in AUX_AT[k]:
                            aux_pass(c - 1, o, aux_ps if u_row else aux_last)
                    if u_row:
                        u1_pass(c, k)
                    if first and k % 3 == 1 and k > 1:
                        z_pass(NB - 1, k // 3 - 1)
                    if first and k == KT - 1:
                        pe.wait_ge(z_ready, NB * TT)
                        pe.wait_ge(mstep, 5)
                        pe.matmul(mean_ps, ones[:], rowsum[:], start=True, stop=True).then_inc(mean_done, 1)

            row2(0, True, False, first=True)
            row2(1, True, True)
            with pe.Fori(2, NB) as c:
                row2(c, True, True)
            row2(NB, False, True)


def kernel(**inputs):
    import numpy as np
    import concourse.bacc as bacc
    from concourse.bass_utils import run_bass_kernel_spmd

    def arr(name):
        return np.asarray(inputs[name])

    x = arr("x")
    x_t = x.transpose(0, 2, 1).reshape(NB, KT, P, S)
    wu1_t = arr("L0_ffn_Wu1").T.reshape(1, KT, P, FU)
    w_t = arr("L0_cond_base_weight").reshape(KT, P, KT, P).transpose(0, 3, 2, 1).reshape(KT, P, D)
    wq_t = arr("L0_ffn_Wq").T.reshape(KT, P, BOT)
    w_all = np.concatenate([w_t, wq_t], axis=2)
    wvu_t = arr("L0_ffn_Wvu").T.reshape(1, P, D)
    wvu_t = np.concatenate([wvu_t, np.zeros((1, P, BOT), np.float32)], axis=2)
    lora_a = arr("L0_cond_lora_A_w")
    na = lora_a.shape[0]
    given = {
        "ids": arr("itok_B_6_15").reshape(1, NB),
        "x": np.concatenate([x_t, wu1_t], axis=0),
        "w": np.concatenate([w_all, wvu_t], axis=0),
        "base_bias": arr("L0_cond_base_bias").reshape(KT, P).T,
        "lora_a": lora_a.reshape(na, RANK, KT, P).transpose(0, 3, 2, 1),
        "lora_b": arr("L0_cond_lora_B_w").reshape(na, TT, S, RANK).transpose(0, 1, 3, 2),
        "wr": arr("L0_ffn_Wr"),
        "wr_t": arr("L0_ffn_Wr").T,
        "keys_t": arr("L0_ffn_aux_keys").T,
        "values_t": arr("L0_ffn_aux_values").T.reshape(KT, P, SLOTS),
        "wvd_t": arr("L0_ffn_Wvd").T.reshape(KT, P, VB).transpose(1, 0, 2),
        "bu1": arr("L0_ffn_bu1").reshape(FT, P).T,
        "wu2": arr("L0_ffn_Wu2").reshape(FT, P).T,
        "bu2": arr("L0_ffn_bu2").reshape(1, 1),
        "gate_w1": arr("L0_ffn_gate_w1").reshape(1, 1),
        "gate_bias": arr("L0_ffn_gate_bias").reshape(1, 1),
        "log_rel": arr("L0_ffn_log_rel").reshape(1, SLOTS),
    }
    nc = bacc.Bacc("TRN2", target_bir_lowering=False, num_devices=1)
    arrays, args = {}, []
    for name, a in given.items():
        a = np.ascontiguousarray(a)
        arrays[f"in_{name}"] = a
        args.append(nc.dram_tensor(f"in_{name}", a.shape, mybir.dt.from_np(a.dtype), kind="ExternalInput").ap())
    out_t = nc.dram_tensor("out_0", (NB, KT, P, S), mybir.dt.float32, kind="ExternalOutput").ap()
    bass_adaln_ffn(nc, *args, out_t)
    r = run_bass_kernel_spmd(nc, [arrays], core_ids=[0])
    got = r.results[0]["out_0"]
    return got.reshape(NB, D, S).transpose(0, 2, 1)
```

```python
import concourse.bass as bass
from concourse import mybir
from contextlib import ExitStack


P = 128
D = 2048
KT = D // P
NB = 8
S = 512
TT = S // P
RANK = 16
REP = 3
KL = REP * 2 * RANK
BOT = 64
RDIM = 48
SLOTS = 512
VB = 128
FU = D // 4
FT = FU // P
NTOK = NB * S
WCOL = D + BOT
WHALF = D // 2
NXR = 8
NTILES = NB * KT
SENTINEL = -3.0e38
MASKED = -1.0e30


def bass_adaln_ffn(
    nc: bass.Bass,
    ids: bass.AP,
    x: bass.AP,
    w: bass.AP,
    base_bias: bass.AP,
    lora_a: bass.AP,
    lora_b: bass.AP,
    wr: bass.AP,
    wr_t: bass.AP,
    keys_t: bass.AP,
    values_t: bass.AP,
    wvd_t: bass.AP,
    bu1: bass.AP,
    wu2: bass.AP,
    bu2: bass.AP,
    gate_w1: bass.AP,
    gate_bias: bass.AP,
    log_rel: bass.AP,
    out: bass.AP,
):
    f32 = mybir.dt.float32
    f32r = mybir.dt.float32r
    ALU = mybir.AluOpType
    ACT = mybir.ActivationFunctionType
    AX = mybir.AxisListType

    h_dram = nc.dram_tensor("h_dram", (NB, KT, P, S), f32, kind="Internal").ap()
    r_dram = nc.dram_tensor("r_dram", (NB, KT, P, S), f32, kind="Internal").ap()

    ctx = ExitStack()
    with ctx:
        def sb(name, shape, dt=f32):
            return ctx.enter_context(nc.sbuf_tensor(name, shape, dt))

        def sem(name):
            return ctx.enter_context(nc.semaphore(name))

        def wait(eng, semaphore, value):
            if isinstance(value, int) and value <= 0:
                return
            eng.wait_ge(semaphore, value)

        xh = sb("xh", [P, KT, S], f32r)
        xl = sb("xl", [P, KT, S], f32r)
        xraw = sb("xraw", [P, NXR, S])
        wraw = sb("wraw", [P, 2, WHALF + BOT])
        wsp = sb("wsp", [P, 2, 2 * WCOL], f32r)
        ids_sb = sb("ids_sb", [1, NB], mybir.dt.int32)
        a_raw = sb("a_raw", [P, KT, RANK])
        a_sp = sb("a_sp", [P, KT, REP, 2, RANK], f32r)
        b_raw = sb("b_raw", [KL, S])
        b_sp = sb("b_sp", [KL, 2, S], f32r)
        ax_sp = sb("ax_sp", [KL, S], f32r)
        stage = sb("stage", [P, 4, S])
        h_sp = sb("h_sp", [P, 2, 2, S], f32r)
        sq = sb("sq", [P, S])
        sum_h = sb("sum_h", [P, S])
        sum_hh = sb("sum_hh", [P, S])
        qa = sb("qa", [P, S], f32r)
        qb = sb("qb", [P, S], f32r)
        rep = sb("rep", [P, S])
        att = sb("att", [P, S])
        wt_sp = sb("wt_sp", [P, 2, TT, 2, P], f32r)
        g_a = sb("g_a", [P, SLOTS], f32r)
        g_b = sb("g_b", [P, SLOTS], f32r)
        k_a = sb("k_a", [P, SLOTS], f32r)
        k_b = sb("k_b", [P, SLOTS], f32r)
        v_sp = sb("v_sp", [P, 2, TT, VB], f32r)
        z_all = sb("z_all", [P, NB, S])
        ident = sb("ident", [P, P])
        ones = sb("ones", [P, P])
        bias_sb = sb("bias_sb", [P, KT])
        bu1_sb = sb("bu1_sb", [P, FT])
        wu2_sb = sb("wu2_sb", [P, FT])
        bu2_sb = sb("bu2_sb", [P, 1])
        bu2_half = sb("bu2_half", [P, 1])
        gw_sb = sb("gw_sb", [P, 1])
        gb_sb = sb("gb_sb", [P, 1])
        gb_half = sb("gb_half", [P, 1])
        gw_half = sb("gw_half", [P, 1])
        top8 = sb("top8", [P, 8])
        nmax = sb("nmax", [P, 1])
        esum = sb("esum", [P, 1])
        rsum = sb("rsum", [P, 1])
        stats = sb("stats", [P, NB, 2, TT])
        mean_t = sb("mean_t", [P, NB, TT])
        var_t = sb("var_t", [P, NB, TT])
        norm_t = sb("norm_t", [P, NB, TT])
        rowsum = sb("rowsum", [P, 1])
        inv_t = sb("inv_t", [P, 1])
        sg = sb("sg", [P, TT])
        un = sb("un", [P, TT])
        gt = sb("gt", [P, TT])
        keep = sb("keep", [P, TT])
        carrier = sb("carrier", [P, 1])

        gact = wraw[:].rearrange("p a n -> p (a n)")[:, 0:FT * S].rearrange("p (m s) -> p m s", m=FT)
        acc = sum_h
        zg = sq
        z_sp = wsp[:, 1, 0:2 * S].rearrange("p (a s) -> p a s", a=2)
        wvu_hi = wsp[:, 0, 0:D]
        wvu_lo = wsp[:, 0, WCOL + BOT:WCOL + BOT + D]
        r_last = [xraw[:, 4 + o, :] for o in range(4)] + [xraw[:, o, :] for o in range(4)] \
            + [z_all[:, b, :] for b in range(NB - 1)] + [rep[:]]
        h_in = xraw[:, 0:4, :]
        r_in = xraw[:, 4:8, :]

        wvd_sb = z_all[:, 4:8, :].rearrange("p b (k v) -> p (b k) v", v=VB)
        values_in = z_all[:, 0:4, :]
        keys_sb = stage[0:BOT, 0, :]
        rk_sb = stage[0:RDIM, 1, :]
        wr_sb = stage[0:RDIM, 2, 0:BOT]
        wrt_sb = stage[0:BOT, 3, 0:RDIM]

        bank = [ctx.enter_context(nc.psum_tensor(f"bank{i}", [P, 512], f32)) for i in range(8)]
        main_ps = bank[0:2]
        q_ps, lora_ps, sc_ps, at_ps, wt_ps, z_ps = bank[2:8]
        stat_ps = z_ps[:, 2 * P:2 * P + 2 * TT]
        aux_last = [bank[4], bank[5], bank[0], bank[1]]
        u_ps = [bank[0], bank[1], bank[3], bank[2]]
        aux_ps = bank[4:6]
        gate_ps = bank[6]
        learned_ps = bank[7][:, 0:TT]
        mean_ps = bank[7][:, 8:9]

        ids_in = sem("ids_in")
        keys_in = sem("keys_in")
        small_in = sem("small_in")
        wvd_in = sem("wvd_in")
        values_ready = [sem(f"values_ready{i}") for i in range(4)]
        raw_in = [sem(f"raw_in{i}") for i in range(NXR)]
        first_in = [sem(f"first_in{i}") for i in range(NXR)]
        w_in = [sem(f"w_in{i}") for i in range(2)]
        a_in = sem("a_in")
        b_in = sem("b_in")
        consts = sem("consts")
        setup_pe = sem("setup_pe")
        setup_act = sem("setup_act")
        setup_dve = sem("setup_dve")
        vslice_used = sem("vslice_used")
        xh_ready = sem("xh_ready")
        xl_ready = sem("xl_ready")
        x_used = sem("x_used")
        wh_ready = sem("wh_ready")
        wl_ready = sem("wl_ready")
        ah_ready = sem("ah_ready")
        al_ready = sem("al_ready")
        bh_ready = sem("bh_ready")
        bl_ready = sem("bl_ready")
        lora_done = sem("lora_done")
        axh_ready = sem("axh_ready")
        ax_ready = sem("ax_ready")
        main_done = sem("main_done")
        h_ready = sem("h_ready")
        sq_ready = sem("sq_ready")
        hh_ready = sem("hh_ready")
        hl_ready = sem("hl_ready")
        h_used = sem("h_used")
        s1_ready = sem("s1_ready")
        s2_ready = sem("s2_ready")
        rx_ready = sem("rx_ready")
        r_ready = sem("r_ready")
        h_out = [sem(f"h_out{i}") for i in range(2)]
        r_out = [sem(f"r_out{i}") for i in range(2)]
        qt_ready = sem("qt_ready")
        qf_ready = sem("qf_ready")
        qh_ready = sem("qh_ready")
        qab_ready = sem("qab_ready")
        stats_done = sem("stats_done")
        stats_ready = sem("stats_ready")
        scores_done = sem("scores_done")
        topk = sem("topk")
        exp_ready = sem("exp_ready")
        rsum_ready = sem("rsum_ready")
        wgt_ready = sem("wgt_ready")
        wt_done = sem("wt_done")
        wth_ready = sem("wth_ready")
        wtl_ready = sem("wtl_ready")
        z_done = sem("z_done")
        z_ready = sem("z_ready")
        mstep = sem("mstep")
        ln_ready = sem("ln_ready")
        mean_done = sem("mean_done")
        u_done = sem("u_done")
        gelu_ready = sem("gelu_ready")
        acc_step = sem("acc_step")
        learned_done = sem("learned_done")
        tanh_ready = sem("tanh_ready")
        gate_step = sem("gate_step")
        gate_done = sem("gate_done")
        zg_ready = sem("zg_ready")
        zgh_ready = sem("zgh_ready")
        zgl_ready = sem("zgl_ready")
        aux_done = sem("aux_done")
        out_ready = sem("out_ready")
        r_tail_in = sem("r_tail_in")
        out_in = [sem(f"out_in{i}") for i in range(4)]

        SUB = ALU.subtract
        TOPK_STEPS = 5
        GATE_STEPS = 8
        X_LOADS = 2 * (NB + 1) - 1

        A_AT = 2
        W_AT = (3, 9)
        QUERY_STEP = 5
        LATE_SLICE = 12
        WVU_STEPS = (12, 14)
        AUX_AT = {k: [] for k in range(KT)}
        for i in range(KT):
            AUX_AT[6 + i // 2 if i < 14 else i - 1].append(i)
        STEP_OF = {o: k for k, os in AUX_AT.items() for o in os}
        EARLY = 10
        LATE_PE = {0: [10, 11], 2: [12, 13], 3: [14], 4: [15]}
        LATE_DVE = {1: [10, 11], 2: [12], 3: [13], 4: [14], 5: [15]}
        LATE_STORE = {1: [10, 11], 3: [12], 4: [13], 5: [14], 6: [15]}

        def x_raw(b, k):
            if isinstance(b, int) and b == 0 and k >= NXR:
                return z_all[:, k - NXR, :]
            return xraw[:, k % NXR, :]

        block = ctx.enter_context(nc.Block())

        @block.sync
        def _(sp):
            sp.dma_start(ids_sb[:], ids).then_inc(ids_in, 16)

            def load_x(b, k):
                sp.dma_start(x_raw(b, k), x[b, k]).then_inc(raw_in[k % NXR], 16)

            def load_w(tile, half):
                n0, n1 = (0, WHALF) if half == 0 else (WHALF, WCOL)
                sp.dma_start(wraw[:, half, 0:n1 - n0], w[tile, :, n0:n1]).then_inc(w_in[half], 16)

            def adapter(b):
                return sp.value_load(ids_sb[0:1, bass.ds(b, 1)], min_val=0, max_val=lora_a.shape[0] - 1)

            def load_b(b, c):
                which = adapter(b)
                wait(sp, bl_ready, b * TT + c)
                for r in range(2 * REP):
                    sp.dma_start(b_raw[r * RANK:(r + 1) * RANK, :], lora_b[which, c]).then_inc(b_in, 16)

            for k in range(KT):
                arrived = raw_in[k] if k < NXR else first_in[k - NXR]
                sp.dma_start(x_raw(0, k), x[0, k]).then_inc(arrived, 16)
                if k == A_AT:
                    sp.wait_ge(ids_in, 16)
                    sp.dma_start(a_raw[:], lora_a[adapter(0)]).then_inc(a_in, 16)
                if k in W_AT:
                    load_w(0, W_AT.index(k))
            load_b(0, 0)
            sp.dma_start(keys_sb, keys_t).then_inc(keys_in, 16)
            sp.dma_start(wr_sb, wr).then_inc(keys_in, 16)
            sp.dma_start(wrt_sb, wr_t).then_inc(keys_in, 16)
            sp.dma_start(rep[BOT:BOT + 1, :], log_rel).then_inc(keys_in, 16)
            sp.dma_start(rep[96:97, :], log_rel).then_inc(keys_in, 16)
            sp.dma_start(bias_sb[:], base_bias).then_inc(small_in, 16)
            sp.dma_start(bu1_sb[:], bu1).then_inc(small_in, 16)
            sp.dma_start(wu2_sb[:], wu2).then_inc(small_in, 16)
            for dst, src in ((bu2_sb, bu2), (gw_sb, gate_w1), (gb_sb, gate_bias)):
                sp.dma_start(dst[:], src.broadcast_to([P, 1])).then_inc(small_in, 16)

            def row(b, last, values=False):
                for o in range(KT):
                    n = b * KT + o
                    if values:
                        if o == 0:
                            sp.wait_ge(xl_ready, KT)
                            sp.dma_start(wvd_sb, wvd_t).then_inc(wvd_in, 16)
                        wait(sp, vslice_used, o - 4 + 1)
                        sp.dma_start(values_in[:, o % 4, :], values_t[o]).then_inc(values_ready[o % 4], 16)
                    tile = (o + 1) % KT if not (last and o == KT - 1) else KT
                    for half in range(2):
                        wait(sp, wl_ready, 2 * n + half + 1)
                        load_w(tile, half)
                    if o == 1 and not last:
                        which = adapter(b + 1)
                        wait(sp, al_ready, b + 1)
                        sp.dma_start(a_raw[:], lora_a[which]).then_inc(a_in, 16)
                    if o % TT == 1 and not (last and o > KT - TT):
                        load_b(b + (o // TT + 1) // TT, (o // TT + 1) % TT)
                    if o == 2:
                        for k in range(NXR):
                            wait(sp, xl_ready, b * KT + k + NXR + 1)
                            load_x(b + 1, k)
                for k in range(NXR, KT):
                    wait(sp, xl_ready, (b + 1) * KT + k - NXR + 1)
                    load_x(b + 1, k)

            row(0, False, values=True)
            row(1, False)
            with sp.Fori(2, NB - 1) as b:
                row(b, False)
            row(NB - 1, True)

            def load_r(c, o):
                if isinstance(c, int) and c == 0 and o < 4:
                    sp.wait_ge(xl_ready, NB * KT + 12 + o + 1)
                else:
                    wait(sp, out_ready, c * KT + o - 4 + 1)
                sp.dma_start(r_in[:, o % 4, :], r_dram[c, o]).then_inc(raw_in[4 + o % 4], 16)

            def load_r_last():
                c = NB - 1
                sp.wait_ge(zg_ready, c)
                for o in range(8, KT):
                    sp.dma_start(r_last[o], r_dram[c, o]).then_inc(r_tail_in, 16)
                for o in range(4, 8):
                    sp.wait_ge(hl_ready, NTILES + c * KT + 12 + o - 4 + 1)
                    sp.dma_start(r_last[o], r_dram[c, o]).then_inc(raw_in[o - 4], 16)
                for o in range(EARLY + 4, KT):
                    load_r(c - 1, o)
                for o in range(4):
                    load_r(c, o)

            def row2(c, h_row, r_row, next_last=False):
                for k in range(KT):
                    if h_row:
                        if isinstance(c, int) and c == 0 and k < 4:
                            sp.wait_ge(xl_ready, NB * KT + 8 + k + 1)
                        else:
                            wait(sp, hl_ready, NTILES + c * KT + k - 4 + 1)
                        sp.dma_start(h_in[:, k % 4, :], h_dram[c, k]).then_inc(raw_in[k % 4], 16)
                    if r_row:
                        for o in range(EARLY + 4 if next_last else KT):
                            if (k == 4 if o < 4 else k == min(KT - 1, STEP_OF[o - 4] + 3)):
                                load_r(c - 1, o)

            for i in range(2):
                sp.wait_ge(h_out[i], 16 * KT // 2)
            row2(0, True, False)
            for i in range(2):
                sp.wait_ge(h_out[i], 16 * NTILES // 2)
                sp.wait_ge(r_out[i], 16 * NTILES // 2)
            row2(1, True, True)
            with sp.Fori(2, NB - 1) as c:
                row2(c, True, True)
            row2(NB - 1, True, True, next_last=True)
            load_r_last()
            for i in range(4):
                sp.wait_ge(out_in[i], 16 * NB * KT // 4)

        @block.gpsimd
        def _(pool):
            filled = ((ones[:], 1.0), (ident[:], 0.0), (qb[BOT:P, :].bitcast(f32), 1.0),
                      (g_b[BOT:P, :].bitcast(f32), 0.0), (k_b[BOT:P, :].bitcast(f32), 0.0))
            for i, (tile, value) in enumerate(filled):
                wait(pool, consts, i)
                pool.memset(tile, value).then_inc(consts, 1)
            pool.wait_ge(consts, 5)
            pool.affine_select(out=ident[:], in_=ident[:], compare_op=ALU.not_equal, fill=1.0, base=0,
                               pattern=[[-1, P]], channel_multiplier=1).then_inc(consts, 1)

        @block.scalar
        def _(act):
            def to_hi(dst, src):
                return act.activation(dst, src, ACT.Copy)

            def split_x_hi(b, k):
                if isinstance(b, int) and b == 0 and k >= NXR:
                    act.wait_ge(first_in[k - NXR], 16)
                elif isinstance(b, int) and b == 0:
                    act.wait_ge(raw_in[k], 16)
                else:
                    wait(act, raw_in[k % NXR], 16 * (2 * b + k // NXR))
                wait(act, x_used, (b - 1) * KT + k + 1)
                wait(act, r_ready, (b - 1) * KT + k + 1)
                to_hi(xh[:, k, :], x_raw(b, k)).then_inc(xh_ready, 1)

            def split_w_hi(m, slot, halves):
                for half in halves:
                    n = WHALF + half * BOT
                    wait(act, w_in[half], 16 * (m + 1))
                    if half == 0:
                        wait(act, h_used, m - 1)
                    to_hi(wsp[:, slot, half * WHALF:half * WHALF + n], wraw[:, half, 0:n])\
                        .then_inc(wh_ready, 1)

            def split_a_hi(b):
                wait(act, a_in, 16 * (b + 1))
                wait(act, lora_done, b)
                for r in range(REP):
                    last = to_hi(a_sp[:, :, r, 0, :], a_raw[:])
                last.then_inc(ah_ready, 1)

            def exp_tile(i):
                wait(act, topk, TOPK_STEPS * (i + 1))
                act.activation(att[:], att[:], ACT.Exp, bias=nmax[:], accum_out=esum[:])\
                    .then_inc(exp_ready, 1)

            def wt_hi(b, t):
                i = b * TT + t
                wait(act, wt_done, i + 1)
                if t % 2 == 0:
                    wait(act, z_done, b * (TT // 2) + t // 2)
                to_hi(wt_sp[:, 0, :, t % 2, :], wt_ps[:].rearrange("p (s t) -> p s t", s=TT))\
                    .then_inc(wth_ready, 1)

            def z_copy(b, t):
                wait(act, z_done, b * (TT // 2) + t // 2 + 1)
                act.activation(z_all[:, b, (t - 1) * P:(t + 1) * P], z_ps[:, 0:2 * P], ACT.Copy)\
                    .then_inc(z_ready, 1)

            def query_hi(b):
                wait(act, h_used, (b + 1) * KT)
                wait(act, wgt_ready, b * TT)
                wait(act, wt_done, b * TT)
                act.activation(att[0:BOT, :], q_ps[BOT:P, :], ACT.Copy).then_inc(qt_ready, 1)
                wait(act, qf_ready, b + 1)
                wait(act, scores_done, b * TT)
                act.activation(qa[0:BOT, :], rep[0:BOT, :], ACT.Copy).then_inc(qh_ready, 1)
                act.activation(qb[0:BOT, :], rep[0:BOT, :], ACT.Copy).then_inc(qh_ready, 1)

            def router_keys_copy():
                act.wait_ge(setup_pe, 1)
                act.activation(rk_sb, main_ps[1][0:RDIM, :], ACT.Copy).then_inc(setup_act, 1)
                act.activation(rep[0:BOT, :], keys_sb, ACT.Copy, scale=float(BOT) ** -0.5)\
                    .then_inc(setup_act, 1)
                act.wait_ge(setup_act, 2)

            def router_factor_copy():
                act.wait_ge(setup_pe, 2)
                act.activation(att[0:BOT, :], q_ps[0:BOT, :], ACT.Copy, scale=float(RDIM) ** -0.5)\
                    .then_inc(setup_act, 1)

            def factors_hi():
                act.wait_ge(keys_in, 80)
                act.wait_ge(setup_act, 3)
                act.wait_ge(consts, 6)
                for dst_a, dst_b, src in ((g_a, g_b, att), (k_a, k_b, rep)):
                    to_hi(dst_a[0:BOT, :], src[0:BOT, :])
                    to_hi(dst_a[BOT:P, :], src[0:BOT, :])
                    to_hi(dst_b[BOT:BOT + 1, :], rep[BOT:BOT + 1, :])
                    to_hi(dst_b[96:97, :], rep[96:97, :]).then_inc(setup_act, 1)
                act.activation(gb_half[:], gb_sb[:], ACT.Copy, scale=0.5)
                act.activation(gw_half[:], gw_sb[:], ACT.Copy, scale=0.5)
                act.activation(bu2_half[:], bu2_sb[:], ACT.Copy, scale=0.5)

            def values_hi():
                act.wait_ge(vslice_used, KT)
                for s in range(TT):
                    last = to_hi(v_sp[:, 0, s, :], bank[4 + s][:, 0:VB])
                last.then_inc(setup_act, 1)

            act.wait_ge(consts, 1)
            act.activation(nmax[:], ones[:, 0:1], ACT.Copy)
            for k in range(KT):
                split_x_hi(0, k)
                if k == A_AT:
                    split_a_hi(0)
                if k in W_AT:
                    split_w_hi(0, 0, (W_AT.index(k),))

            def store_h(b, o):
                act.dma_start(h_dram[b, o], stage[:, o % 2, :]).then_inc(h_out[o % 2], 16)

            def store_r(b, o):
                wait(act, r_ready, b * KT + o + 1)
                act.dma_start(r_dram[b, o], stage[:, 2 + o % 2, :]).then_inc(r_out[o % 2], 16)

            def row(b, first, last):
                wait(act, lora_done, b + 1)
                wait(act, main_done, b * KT)
                to_hi(ax_sp[:], lora_ps[0:KL, :]).then_inc(axh_ready, 1)
                for o in range(KT):
                    n = b * KT + o
                    t = o // TT
                    if not first and o % TT == 3:
                        wt_hi(b - 1, t)
                    if o == KT - 1:
                        for k in range(LATE_SLICE if last else KT - 1):
                            split_x_hi(b + 1, k)
                    if o % TT == 0:
                        wait(act, b_in, 2 * REP * 16 * (b * TT + t + 1))
                        wait(act, main_done, n - TT)
                        to_hi(b_sp[:, t % 2, :], b_raw[:]).then_inc(bh_ready, 1)
                    if first and o == 0:
                        router_keys_copy()
                    if o < KT - 1:
                        split_w_hi(n + 1, (o + 1) % 2, (0, 1))
                    if o == 0 and not first:
                        query_hi(b - 1)
                    if not first and o % TT == 1:
                        exp_tile((b - 1) * TT + t)
                    if o == 2 and not last:
                        split_a_hi(b + 1)
                    if first and o == 2:
                        factors_hi()
                    slot = o % 2
                    wait(act, main_done, n + 1)
                    wait(act, hl_ready, n - 1)
                    wait(act, h_out[slot], 16 * (b * (KT // 2) + o // 2))
                    if first and o == 0:
                        act.wait_ge(small_in, 96)
                    act.activation(stage[:, slot, :], main_ps[slot][:], ACT.Identity,
                                   bias=bias_sb[:, o:o + 1]).then_inc(h_ready, 1)
                    wait(act, h_used, n - 1)
                    wait(act, h_ready, n + 1)
                    to_hi(h_sp[:, slot, 0, :], stage[:, slot, :]).then_inc(hh_ready, 1)
                    if first and o == 0:
                        router_factor_copy()
                    if o == KT - 1 and not last:
                        split_w_hi(n + 1, 0, (0,))
                        split_x_hi(b + 1, KT - 1)
                        split_w_hi(n + 1, 0, (1,))
                    wait(act, s2_ready, n)
                    act.activation(sq[:], stage[:, slot, :], ACT.Square).then_inc(sq_ready, 1)
                    store_h(b, o)
                    if o > 0:
                        store_r(b, o - 1)
                    if not first and o % TT == 3 and t % 2 == 1:
                        z_copy(b - 1, t)
                if not last:
                    store_r(b, KT - 1)

            row(0, True, False)
            values_hi()
            row(1, False, False)
            with act.Fori(2, NB - 1) as b:
                row(b, False, False)
            row(NB - 1, False, True)

            def h_hi(c, k):
                m = c * KT + k
                wait(act, raw_in[k % 4], 16 * (X_LOADS + c * (KT // 4) + k // 4 + 1))
                wait(act, h_used, NTILES + m - 1)
                to_hi(h_sp[:, k % 2, 0, :], h_in[:, k % 4, :]).then_inc(hh_ready, 1)

            def gelus(c):
                wait(act, acc_step, c * FT)
                for m in range(FT):
                    if m < FT - 1:
                        wait(act, u_done, (FT - 1) * c + m + 1)
                    else:
                        wait(act, h_used, NTILES + (c + 1) * KT)
                    act.activation(gact[:, m, :], u_ps[m][:], ACT.Gelu_apprx_tanh,
                                   bias=bu1_sb[:, m:m + 1]).then_inc(gelu_ready, 1)

            def store_out(c, o):
                wait(act, out_ready, c * KT + o + 1)
                tile = r_last[o] if isinstance(c, int) and c == NB - 1 else stage[:, o % 4, :]
                act.dma_start(out[c, o], tile).then_inc(out_in[o % 4], 16)

            def gate_act(c, k):
                if k == 2:
                    wait(act, learned_done, c + 1)
                    wait(act, gate_step, GATE_STEPS * c)
                    act.activation(sg[:], learned_ps, ACT.Tanh, bias=bu2_half[:], scale=0.5)\
                        .then_inc(tanh_ready, 1)
                if k == 3:
                    wait(act, gate_step, GATE_STEPS * c + 5)
                    wait(act, gate_done, c)
                    act.activation(gt[:], un[:], ACT.Tanh, bias=gb_half[:], scale=gw_half[:])\
                        .then_inc(tanh_ready, 1)
                if k == 5:
                    wait(act, zg_ready, c + 1)
                    wait(act, aux_done, c * KT)
                    to_hi(z_sp[:, 0, :], zg[:]).then_inc(zgh_ready, 1)

            def row2(c, u_row, aux_row, first=False):
                count = EARLY if isinstance(c, int) and c == NB - 1 else KT
                for k in range(KT):
                    if u_row:
                        h_hi(c, k)
                    if first:
                        if k == 0:
                            query_hi(NB - 1)
                        if k == 2:
                            store_r(NB - 1, KT - 1)
                        if k < KT - LATE_SLICE:
                            split_x_hi(NB, LATE_SLICE + k)
                        if k % 3 == 1 and k > 1:
                            wt_hi(NB - 1, k // 3 - 1)
                        if k in (8, 14):
                            z_copy(NB - 1, k // 3 - 1)
                        if k % 3 == 0 and k > 0 and k < 13:
                            exp_tile((NB - 1) * TT + k // 3 - 1)
                        if k in WVU_STEPS:
                            split_w_hi(NTILES, 0, (WVU_STEPS.index(k),))
                        if k == 13:
                            wait(act, mstep, 4)
                            act.activation(norm_t[:], var_t[:], ACT.Ln, bias=1.0).then_inc(ln_ready, 1)
                    if aux_row:
                        if k == 0:
                            gelus(c - 1)
                        gate_act(c - 1, k)
                        if not u_row:
                            for o in LATE_STORE.get(k, []):
                                store_out(c - 2, o)
                        for o in AUX_AT[k]:
                            if 0 < o < count:
                                store_out(c - 1, o - 1)
                if aux_row:
                    store_out(c - 1, count - 1)

            row2(0, True, False, first=True)
            row2(1, True, True)
            with act.Fori(2, NB - 1) as c:
                row2(c, True, True)
            row2(NB - 1, True, True)
            row2(NB, False, True)

        @block.vector
        def _(dve):
            def lo(dst, src, hi):
                return dve.tensor_tensor(dst, src, hi.bitcast(f32), SUB)

            def split_x_lo(b, k):
                wait(dve, xh_ready, b * KT + k + 1)
                lo(xl[:, k, :], x_raw(b, k), xh[:, k, :]).then_inc(xl_ready, 1)

            def split_w_lo(m, slot, halves=(0, 1)):
                if 0 in halves:
                    wait(dve, wh_ready, 2 * m + 1)
                    lo(wsp[:, slot, WCOL + BOT:WCOL + BOT + WHALF], wraw[:, 0, 0:WHALF],
                       wsp[:, slot, 0:WHALF]).then_inc(wl_ready, 1)
                if 1 in halves:
                    wait(dve, wh_ready, 2 * m + 2)
                    lo(wsp[:, slot, WCOL:WCOL + BOT], wraw[:, 1, WHALF:WHALF + BOT], wsp[:, slot, D:WCOL])
                    lo(wsp[:, slot, WCOL + BOT + WHALF:2 * WCOL], wraw[:, 1, 0:WHALF],
                       wsp[:, slot, WHALF:D]).then_inc(wl_ready, 1)

            def split_a_lo(b):
                wait(dve, ah_ready, b + 1)
                for r in range(REP):
                    last = lo(a_sp[:, :, r, 1, :], a_raw[:], a_sp[:, :, r, 0, :])
                last.then_inc(al_ready, 1)

            def carry():
                dve.memset(carrier[:], 0.0)

            def top_eight(i):
                selected(i)
                masked(i)

            def selected(i):
                wait(dve, scores_done, i + 1)
                carry()
                dve.max(top8[:], sc_ps[:]).then_inc(topk, 1)
                wait(dve, topk, TOPK_STEPS * i + 1)
                carry()
                dve.match_replace(rep[:], top8[:], sc_ps[:], SENTINEL).then_inc(topk, 1)

            def masked(i):
                wait(dve, topk, TOPK_STEPS * i + 2)
                dve.tensor_scalar(rep[:], rep[:], SENTINEL, MASKED, ALU.not_equal, ALU.mult)\
                    .then_inc(topk, 1)
                wait(dve, topk, TOPK_STEPS * i + 3)
                wait(dve, wt_done, i)
                dve.tensor_tensor(att[:], at_ps[:], rep[:], ALU.add).then_inc(topk, 1)
                wait(dve, topk, TOPK_STEPS * i + 4)
                dve.tensor_reduce(nmax[:], att[:], AX.X, ALU.max, negate=True).then_inc(topk, 1)

            def normalise(i):
                wait(dve, exp_ready, i + 1)
                dve.reciprocal(rsum[:], esum[:]).then_inc(rsum_ready, 1)
                wait(dve, rsum_ready, i + 1)
                dve.tensor_scalar(att[:], att[:], rsum[:], None, ALU.mult).then_inc(wgt_ready, 1)

            def wt_lo(b, t):
                wait(dve, wth_ready, b * TT + t + 1)
                lo(wt_sp[:, 1, :, t % 2, :], wt_ps[:].rearrange("p (s t) -> p s t", s=TT),
                   wt_sp[:, 0, :, t % 2, :])\
                    .then_inc(wtl_ready, 1)

            def query_lo(b):
                wait(dve, qt_ready, b + 1)
                dve.tensor_tensor(rep[0:BOT, :], q_ps[0:BOT, :], att[0:BOT, :], ALU.add)\
                    .then_inc(qf_ready, 1)
                wait(dve, qh_ready, 2 * b + 1)
                wait(dve, qf_ready, b + 1)
                lo(qa[BOT:P, :], rep[0:BOT, :], qa[0:BOT, :]).then_inc(qab_ready, 1)

            def copy_stats(b):
                wait(dve, stats_done, b + 1)
                dve.tensor_copy(stats[:, b, :, :], stat_ps.rearrange("p (a t) -> p a t", a=2))\
                    .then_inc(stats_ready, 1)

            def factors_lo():
                dve.wait_ge(setup_act, 4)
                lo(g_b[0:BOT, :], att[0:BOT, :], g_a[0:BOT, :])
                lo(g_b[96:97, :], rep[96:97, :], g_b[96:97, :]).then_inc(setup_dve, 1)
                dve.wait_ge(setup_act, 5)
                lo(k_b[0:BOT, :], rep[0:BOT, :], k_a[0:BOT, :])
                lo(k_b[96:97, :], rep[96:97, :], k_b[96:97, :]).then_inc(setup_dve, 1)

            def values_lo():
                dve.wait_ge(setup_act, 6)
                for s in range(TT):
                    last = lo(v_sp[:, 1, s, :], bank[4 + s][:, 0:VB], v_sp[:, 0, s, :])
                last.then_inc(setup_dve, 1)

            for k in range(KT):
                split_x_lo(0, k)
                if k == A_AT:
                    split_a_lo(0)
                if k in W_AT:
                    split_w_lo(0, 0, (W_AT.index(k),))

            def residual(b, o):
                n = b * KT + o
                slot = o % 2
                h_tile = stage[:, slot, :]
                r_tile = stage[:, 2 + slot, :]
                wait(dve, h_ready, n + 1)
                wait(dve, r_out[slot], 16 * (b * (KT // 2) + o // 2))
                dve.tensor_tensor(r_tile, h_tile, xl[:, o, :].bitcast(f32), ALU.add)\
                    .then_inc(rx_ready, 1)
                wait(dve, rx_ready, n + 1)
                dve.tensor_tensor(r_tile, r_tile, xh[:, o, :].bitcast(f32), ALU.add)\
                    .then_inc(r_ready, 1)

            def row(b, first, last):
                wait(dve, axh_ready, b + 1)
                lo(ax_sp[2 * RANK:4 * RANK, :], lora_ps[2 * RANK:4 * RANK, :],
                   ax_sp[2 * RANK:4 * RANK, :]).then_inc(ax_ready, 1)
                for o in range(KT):
                    n = b * KT + o
                    t = o // TT
                    slot = o % 2
                    if not first and o % TT == 1:
                        top_eight((b - 1) * TT + t)
                    if not first and o % TT == 3:
                        wt_lo(b - 1, t)
                    if o == KT - 1:
                        for k in range(LATE_SLICE if last else KT - 1):
                            split_x_lo(b + 1, k)
                    if o % TT == 0:
                        wait(dve, bh_ready, b * TT + t + 1)
                        lo(b_sp[4 * RANK:KL, t % 2, :], b_raw[4 * RANK:KL, :], b_sp[4 * RANK:KL, t % 2, :])\
                            .then_inc(bl_ready, 1)
                    if o < KT - 1:
                        split_w_lo(n + 1, (o + 1) % 2)
                    if o == 0 and not first:
                        copy_stats(b - 1)
                        query_lo(b - 1)
                    if not first and o % TT == 1:
                        normalise((b - 1) * TT + t)
                    if o == 2 and not last:
                        split_a_lo(b + 1)
                    if first and o == 2:
                        factors_lo()
                    h_tile = stage[:, slot, :]
                    if first and o == 0:
                        dve.wait_ge(setup_pe, 2)
                    if not (last and o == KT - 1):
                        residual(b, o)
                    if o == KT - 1 and not last:
                        split_w_lo(n + 1, 0, (0,))
                        split_x_lo(b + 1, KT - 1)
                    if o == 0:
                        wait(dve, stats_done, b)
                        dve.tensor_copy(sum_h[:], h_tile).then_inc(s1_ready, 1)
                    else:
                        wait(dve, h_ready, n + 1)
                        wait(dve, s1_ready, n)
                        dve.tensor_tensor(sum_h[:], sum_h[:], h_tile, ALU.add).then_inc(s1_ready, 1)
                    wait(dve, hh_ready, n + 1)
                    lo(h_sp[:, slot, 1, :], h_tile, h_sp[:, slot, 0, :]).then_inc(hl_ready, 1)
                    if o == KT - 1 and not last:
                        split_w_lo(n + 1, 0, (1,))
                    wait(dve, sq_ready, n + 1)
                    if o == 0:
                        dve.tensor_copy(sum_hh[:], sq[:]).then_inc(s2_ready, 1)
                    else:
                        wait(dve, s2_ready, n)
                        dve.tensor_tensor(sum_hh[:], sum_hh[:], sq[:], ALU.add).then_inc(s2_ready, 1)

            row(0, True, False)
            values_lo()
            row(1, False, False)
            with dve.Fori(2, NB - 1) as b:
                row(b, False, False)
            row(NB - 1, False, True)

            def variances():
                dve.wait_ge(stats_ready, NB)
                dve.tensor_scalar(mean_t[:], stats[:, :, 0, :], 1.0 / D, None, ALU.mult).then_inc(mstep, 1)
                dve.wait_ge(mstep, 1)
                dve.tensor_tensor(mean_t[:], mean_t[:], mean_t[:], ALU.mult).then_inc(mstep, 1)
                dve.wait_ge(mstep, 2)
                dve.scalar_tensor_tensor(var_t[:], stats[:, :, 1, :], 1.0 / D, mean_t[:], ALU.mult, SUB)\
                    .then_inc(mstep, 1)
                dve.wait_ge(mstep, 3)
                dve.tensor_scalar(var_t[:], var_t[:], 0.0, None, ALU.max).then_inc(mstep, 1)

            def sum_of_logs():
                dve.wait_ge(ln_ready, 1)
                dve.tensor_reduce(rowsum[:], norm_t[:].rearrange("p b t -> p (b t)"), AX.X, ALU.add)\
                    .then_inc(mstep, 1)

            def mean_of_logs():
                dve.wait_ge(mean_done, 1)
                dve.tensor_scalar(inv_t[:], mean_ps, 1.0 / NTOK, 1e-6, ALU.mult, ALU.add).then_inc(mstep, 1)
                dve.wait_ge(mstep, 6)
                dve.reciprocal(inv_t[:], inv_t[:]).then_inc(mstep, 1)
                dve.wait_ge(mstep, 7)
                dve.tensor_scalar(norm_t[:], norm_t[:], inv_t[:], 0.5, ALU.mult, ALU.mult).then_inc(mstep, 1)

            def gate_dve(c, k):
                step = GATE_STEPS * c
                if k < 2:
                    if k == 0:
                        wait(dve, learned_done, c)
                    for m in range(k * FT // 2, (k + 1) * FT // 2):
                        wait(dve, gelu_ready, c * FT + m + 1)
                        if m == 0:
                            dve.tensor_scalar(acc[:], gact[:, 0, :], wu2_sb[:, 0:1], None, ALU.mult)\
                                .then_inc(acc_step, 1)
                        else:
                            wait(dve, acc_step, c * FT + m)
                            dve.scalar_tensor_tensor(acc[:], gact[:, m, :], wu2_sb[:, m:m + 1], acc[:],
                                                     ALU.mult, ALU.add).then_inc(acc_step, 1)
                if k == 2:
                    wait(dve, tanh_ready, 2 * c + 1)
                    dve.tensor_scalar(un[:], sg[:], 1.25, 1.25, ALU.mult, ALU.add).then_inc(gate_step, 1)
                    wait(dve, gate_step, step + 1)
                    dve.tensor_tensor(un[:], un[:], norm_t[:, c, :], ALU.add).then_inc(gate_step, 1)
                    wait(dve, gate_step, step + 2)
                    dve.tensor_scalar(un[:], un[:], 0.0, 5.0, ALU.max, ALU.min).then_inc(gate_step, 1)
                    wait(dve, gate_step, step + 3)
                    dve.tensor_scalar(un[:], un[:], 0.5, 1.0 / 1.5, SUB, ALU.mult).then_inc(gate_step, 1)
                    wait(dve, gate_step, step + 4)
                    dve.tensor_scalar(un[:], un[:], 0.0, 1.0, ALU.max, ALU.min).then_inc(gate_step, 1)
                if k == 3:
                    wait(dve, tanh_ready, 2 * c + 2)
                    dve.tensor_scalar(gt[:], gt[:], 0.5, 0.5, ALU.mult, ALU.add).then_inc(gate_step, 1)
                    wait(dve, gate_step, step + 6)
                    dve.tensor_scalar(keep[:], gt[:], 0.05, None, ALU.is_ge).then_inc(gate_step, 1)
                    wait(dve, gate_step, step + 7)
                    dve.tensor_tensor(gt[:], gt[:], keep[:], ALU.mult).then_inc(gate_step, 1)
                if k == 4:
                    wait(dve, gate_done, c + 1)
                    wait(dve, zgl_ready, c)
                    dve.tensor_tensor(zg[:], gate_ps[:], z_all[:, c, :], ALU.mult).then_inc(zg_ready, 1)
                if k == 5:
                    wait(dve, zgh_ready, c + 1)
                    lo(z_sp[:, 1, :], zg[:], z_sp[:, 0, :]).then_inc(zgl_ready, 1)

            def add_out_last(o):
                c = NB - 1
                wait(dve, aux_done, c * KT + o + 1)
                if o < 8:
                    rows = c * (KT // 4) if o < 4 else NB * (KT // 4)
                    wait(dve, raw_in[(4 + o) % 8], 16 * (X_LOADS + rows + 1))
                elif o == 8:
                    dve.wait_ge(r_tail_in, 16 * 8)
                dve.tensor_tensor(r_last[o], aux_last[o % 4][:], r_last[o], ALU.add)\
                    .then_inc(out_ready, 1)

            def add_out(c, o):
                wait(dve, aux_done, c * KT + o + 1)
                wait(dve, raw_in[4 + o % 4], 16 * (X_LOADS + c * (KT // 4) + o // 4 + 1))
                wait(dve, out_in[o % 4], 16 * (c * (KT // 4) + o // 4))
                dve.tensor_tensor(stage[:, o % 4, :], aux_ps[o % 2][:], r_in[:, o % 4, :], ALU.add)\
                    .then_inc(out_ready, 1)

            def row2(c, u_row, aux_row, first=False):
                count = EARLY if isinstance(c, int) and c == NB - 1 else KT
                for k in range(KT):
                    if u_row:
                        m = NTILES + c * KT + k
                        wait(dve, hh_ready, m + 1)
                        lo(h_sp[:, k % 2, 1, :], h_in[:, k % 4, :], h_sp[:, k % 2, 0, :])\
                            .then_inc(hl_ready, 1)
                    if first:
                        if k == 0:
                            query_lo(NB - 1)
                        if k == 1:
                            residual(NB - 1, KT - 1)
                            copy_stats(NB - 1)
                        if k < KT - LATE_SLICE:
                            split_x_lo(NB, LATE_SLICE + k)
                        if k == 3:
                            variances()
                        if k % 3 == 1 and k > 1:
                            wt_lo(NB - 1, k // 3 - 1)
                        if k % 3 == 1 and k < 12:
                            selected((NB - 1) * TT + k // 3)
                        if k % 3 == 2 and k < 12:
                            masked((NB - 1) * TT + k // 3)
                        if k % 3 == 0 and k > 0 and k < 13:
                            normalise((NB - 1) * TT + k // 3 - 1)
                        if k in WVU_STEPS:
                            split_w_lo(NTILES, 0, (WVU_STEPS.index(k),))
                        if k == 14:
                            sum_of_logs()
                        if k == 15:
                            mean_of_logs()
                            for i in range(2):
                                dve.wait_ge(h_out[i], 16 * NTILES // 2)
                                dve.wait_ge(r_out[i], 16 * NTILES // 2)
                    if aux_row:
                        gate_dve(c - 1, k)
                        if not u_row:
                            for o in LATE_DVE.get(k, []):
                                add_out(c - 2, o)
                        for o in AUX_AT[k]:
                            if not u_row:
                                add_out_last(o)
                            elif o < count:
                                add_out(c - 1, o)

            row2(0, True, False, first=True)
            row2(1, True, True)
            with dve.Fori(2, NB - 1) as c:
                row2(c, True, True)
            row2(NB - 1, True, True)
            row2(NB, False, True)

        @block.tensor
        def _(pe):
            def router_keys():
                pe.wait_ge(keys_in, 80)
                pe.matmul(main_ps[1][0:RDIM, :], wrt_sb, keys_sb, start=True, stop=True)\
                    .then_inc(setup_pe, 1)

            def router_factor():
                pe.wait_ge(setup_act, 1)
                pe.matmul(q_ps[0:BOT, :], wr_sb, rk_sb, start=True, stop=True).then_inc(setup_pe, 1)

            def values_pass(k):
                if k == 0:
                    pe.wait_ge(wvd_in, 16)
                pe.wait_ge(values_ready[k % 4], 16 * (k // 4 + 1))
                for s in range(TT):
                    last = pe.matmul(bank[4 + s][:, 0:VB], values_in[:, k % 4, s * P:(s + 1) * P],
                                     wvd_sb[:, k, :], start=(k == 0), stop=(k == KT - 1))
                last.then_inc(vslice_used, 1)

            def lora_a_step(b, k):
                if k == 0:
                    wait(pe, al_ready, b + 1)
                    wait(pe, ax_ready, b)
                wait(pe, xl_ready, b * KT + k + 1)
                a_k = a_sp[:, k, :, :, :].rearrange("p r a n -> p (r a n)")
                pe.matmul(lora_ps[0:KL, :], a_k, xh[:, k, :], start=(k == 0), stop=False)
                last = pe.matmul(lora_ps[0:KL, :], a_k, xl[:, k, :], start=False, stop=(k == KT - 1))
                if k == KT - 1:
                    last.then_inc(lora_done, 1)

            def query_pass(n, o):
                slot = o % 2
                wait(pe, hl_ready, n + 1)
                wq = wsp[:, slot, D:D + 2 * BOT]
                pe.matmul(q_ps[:], wq, h_sp[:, slot, 0, :], start=(o == 0), stop=False)
                pe.matmul(q_ps[:], wq, h_sp[:, slot, 1, :], start=False, stop=(o == KT - 1)).then_inc(h_used, 1)

            def stats_pass(b):
                wait(pe, s2_ready, (b + 1) * KT)
                wait(pe, z_ready, b * (TT // 2))
                for i, s in enumerate((sum_h, sum_hh)):
                    for t in range(TT):
                        last = pe.matmul(stat_ps[:, i * TT + t:i * TT + t + 1], s[:, t * P:(t + 1) * P],
                                         ones[:, 0:1], start=True, stop=True)
                last.then_inc(stats_done, 1)

            def scores(b, t):
                i = b * TT + t
                if t == 0:
                    wait(pe, qab_ready, b + 1)
                    wait(pe, qh_ready, 2 * b + 2)
                wait(pe, topk, TOPK_STEPS * i)
                tok = slice(t * P, (t + 1) * P)
                pe.matmul(sc_ps[:], qa[:, tok], g_a[:], start=True, stop=False)
                pe.matmul(sc_ps[:], qb[:, tok], g_b[:], start=False, stop=True)
                pe.matmul(at_ps[:], qa[:, tok], k_a[:], start=True, stop=False)
                pe.matmul(at_ps[:], qb[:, tok], k_b[:], start=False, stop=True).then_inc(scores_done, 1)

            def transposes(i):
                wait(pe, wgt_ready, i + 1)
                wait(pe, wtl_ready, i)
                for s in range(TT):
                    last = pe.transpose(wt_ps[:, s * P:(s + 1) * P], att[:, s * P:(s + 1) * P], ident[:])
                last.then_inc(wt_done, 1)

            def z_pass(b, t):
                wait(pe, wtl_ready, b * TT + t + 1)
                wait(pe, z_ready, b * (TT // 2) + t // 2)
                if t == 1:
                    wait(pe, stats_ready, b + 1)
                parts = [(0, 0), (0, 1), (1, 0)]
                for s in range(TT):
                    for j, (v, m) in enumerate(parts):
                        last = pe.matmul(z_ps[:, 0:2 * P], v_sp[:, v, s, :], wt_sp[:, m, s, :, :],
                                         start=(s == 0 and j == 0), stop=(s == TT - 1 and j == 2))
                last.then_inc(z_done, 1)

            def row(b, first, last):
                for o in range(KT):
                    n = b * KT + o
                    t = o // TT
                    slot = o % 2
                    acc_ps = main_ps[slot][:]
                    if not first and o % TT == 1:
                        scores(b - 1, t)
                    if not first and o % TT == 3:
                        transposes((b - 1) * TT + t)
                    wait(pe, h_ready, n - 1)
                    for k in range(KT):
                        if first and o == 0:
                            lora_a_step(0, k)
                        if k % (KT // 2) == 0:
                            wait(pe, wl_ready, 2 * n + k // (KT // 2) + 1)
                        w_hi = wsp[:, slot, k * P:(k + 1) * P]
                        w_lo = wsp[:, slot, WCOL + BOT + k * P:WCOL + BOT + (k + 1) * P]
                        pe.matmul(acc_ps, w_hi, xh[:, k, :], start=(k == 0), stop=False)
                        pe.matmul(acc_ps, w_hi, xl[:, k, :], start=False, stop=False)
                        last_k = pe.matmul(acc_ps, w_lo, xh[:, k, :], start=False, stop=False)
                        if o == KT - 1:
                            last_k.then_inc(x_used, 1)
                        if k == QUERY_STEP and not (first and o == 0):
                            if o == 1:
                                wait(pe, qf_ready, b)
                                if first:
                                    pe.wait_ge(setup_act, 3)
                            query_pass(n - 1, (o - 1) % KT)
                            if o == 0:
                                stats_pass(b - 1)
                    if first and o == 0:
                        router_keys()
                    if o == 0:
                        wait(pe, ax_ready, b + 1)
                    if o % TT == 0:
                        wait(pe, bl_ready, b * TT + t + 1)
                    pe.matmul(acc_ps, b_sp[:, t % 2, (o % TT) * P:(o % TT + 1) * P], ax_sp[:],
                              start=False, stop=True).then_inc(main_done, 1)
                    if first:
                        if o == 0:
                            router_factor()
                        values_pass(o)
                    if not first and o % TT == 3 and t % 2 == 1:
                        z_pass(b - 1, t)
                if not last:
                    for k in range(KT):
                        lora_a_step(b + 1, k)
                if first:
                    pe.wait_ge(setup_dve, 3)

            row(0, True, False)
            row(1, False, False)
            with pe.Fori(2, NB - 1) as b:
                row(b, False, False)
            row(NB - 1, False, True)

            def u1_pass(c, k):
                m0 = NTILES + c * KT + k
                slot = k % 2
                wait(pe, hl_ready, m0 + 1)
                if isinstance(c, int) and c == 0:
                    pe.wait_ge(xl_ready, NB * KT + k + 1)
                for m in range(FT):
                    if k == 0:
                        if isinstance(c, int) and c == 0:
                            if m == 0:
                                pe.wait_ge(h_ready, NTILES)
                            if m == 3:
                                pe.wait_ge(qf_ready, NB)
                        else:
                            wait(pe, gelu_ready, (c - 1) * FT + m + 1)
                    f = slice(m * P, (m + 1) * P)
                    pe.matmul(u_ps[m][:], xh[:, k, f], h_sp[:, slot, 0, :], start=(k == 0), stop=False)
                    pe.matmul(u_ps[m][:], xh[:, k, f], h_sp[:, slot, 1, :], start=False, stop=False)
                    last = pe.matmul(u_ps[m][:], xl[:, k, f], h_sp[:, slot, 0, :], start=False,
                                     stop=(k == KT - 1))
                    if k == KT - 1 and m < FT - 1:
                        last.then_inc(u_done, 1)
                last.then_inc(h_used, 1)

            def learned_pass(c):
                wait(pe, acc_step, (c + 1) * FT)
                wait(pe, tanh_ready, 2 * c)
                for t in range(TT):
                    last = pe.matmul(learned_ps[:, t:t + 1], acc[:, t * P:(t + 1) * P], ones[:, 0:1],
                                     start=True, stop=True)
                last.then_inc(learned_done, 1)

            def gate_pass(c):
                wait(pe, gate_step, GATE_STEPS * (c + 1))
                wait(pe, zg_ready, c)
                for t in range(TT):
                    last = pe.transpose(gate_ps[:, t * P:(t + 1) * P],
                                        gt[:, t:t + 1].broadcast_to([P, P]), ident[:])
                last.then_inc(gate_done, 1)

            def aux_pass(c, o, banks):
                if o == 0:
                    wait(pe, zgl_ready, c + 1)
                if banks is aux_ps or o < 2:
                    wait(pe, out_ready, c * KT + o - 1)
                elif o >= 4:
                    wait(pe, out_ready, c * KT + o - 3)
                ps = banks[o % len(banks)][:]
                f = slice(o * P, (o + 1) * P)
                pe.matmul(ps, wvu_hi[:, f], z_sp[:, 0, :], start=True, stop=False)
                pe.matmul(ps, wvu_hi[:, f], z_sp[:, 1, :], start=False, stop=False)
                pe.matmul(ps, wvu_lo[:, f], z_sp[:, 0, :], start=False, stop=True).then_inc(aux_done, 1)

            def row2(c, u_row, aux_row, first=False):
                count = EARLY if isinstance(c, int) and c == NB - 1 else KT
                for k in range(KT):
                    if first and k == 0:
                        query_pass(NTILES - 1, KT - 1)
                    if first and k == 1:
                        stats_pass(NB - 1)
                    if first and k % 3 == 1 and k > 1:
                        transposes((NB - 1) * TT + k // 3 - 1)
                    if first and k % 3 == 1 and k < 12:
                        scores(NB - 1, k // 3)
                    if aux_row:
                        if k == 2:
                            learned_pass(c - 1)
                        if k == 4:
                            gate_pass(c - 1)
                        if not u_row:
                            for o in LATE_PE.get(k, []):
                                aux_pass(c - 2, o, aux_ps)
                        for o in AUX_AT[k]:
                            if o < count:
                                aux_pass(c - 1, o, aux_ps if u_row else aux_last)
                    if first and k == KT - 1:
                        pe.wait_ge(z_ready, NB * TT // 2)
                        pe.wait_ge(mstep, 5)
                        pe.matmul(mean_ps, ones[:], rowsum[:], start=True, stop=True).then_inc(mean_done, 1)
                    if u_row:
                        u1_pass(c, k)
                    if first and k in (7, 13):
                        z_pass(NB - 1, k // 3 - 1)

            row2(0, True, False, first=True)
            row2(1, True, True)
            with pe.Fori(2, NB - 1) as c:
                row2(c, True, True)
            row2(NB - 1, True, True)
            row2(NB, False, True)


def kernel(**inputs):
    import numpy as np
    import concourse.bacc as bacc
    from concourse.bass_utils import run_bass_kernel_spmd

    def arr(name):
        return np.asarray(inputs[name])

    x = arr("x")
    x_t = x.transpose(0, 2, 1).reshape(NB, KT, P, S)
    wu1_t = arr("L0_ffn_Wu1").T.reshape(1, KT, P, FU)
    w_t = arr("L0_cond_base_weight").reshape(KT, P, KT, P).transpose(0, 3, 2, 1).reshape(KT, P, D)
    wq_t = arr("L0_ffn_Wq").T.reshape(KT, P, BOT)
    w_all = np.concatenate([w_t, wq_t], axis=2)
    wvu_t = arr("L0_ffn_Wvu").T.reshape(1, P, D)
    wvu_t = np.concatenate([wvu_t, np.zeros((1, P, BOT), np.float32)], axis=2)
    lora_a = arr("L0_cond_lora_A_w")
    na = lora_a.shape[0]
    given = {
        "ids": arr("itok_B_6_15").reshape(1, NB),
        "x": np.concatenate([x_t, wu1_t], axis=0),
        "w": np.concatenate([w_all, wvu_t], axis=0),
        "base_bias": arr("L0_cond_base_bias").reshape(KT, P).T,
        "lora_a": lora_a.reshape(na, RANK, KT, P).transpose(0, 3, 2, 1),
        "lora_b": arr("L0_cond_lora_B_w").reshape(na, TT, S, RANK).transpose(0, 1, 3, 2),
        "wr": arr("L0_ffn_Wr"),
        "wr_t": arr("L0_ffn_Wr").T,
        "keys_t": arr("L0_ffn_aux_keys").T,
        "values_t": arr("L0_ffn_aux_values").T.reshape(KT, P, SLOTS),
        "wvd_t": arr("L0_ffn_Wvd").T.reshape(KT, P, VB).transpose(1, 0, 2),
        "bu1": arr("L0_ffn_bu1").reshape(FT, P).T,
        "wu2": arr("L0_ffn_Wu2").reshape(FT, P).T,
        "bu2": arr("L0_ffn_bu2").reshape(1, 1),
        "gate_w1": arr("L0_ffn_gate_w1").reshape(1, 1),
        "gate_bias": arr("L0_ffn_gate_bias").reshape(1, 1),
        "log_rel": arr("L0_ffn_log_rel").reshape(1, SLOTS),
    }
    nc = bacc.Bacc("TRN2", target_bir_lowering=False, num_devices=1)
    arrays, args = {}, []
    for name, a in given.items():
        a = np.ascontiguousarray(a)
        arrays[f"in_{name}"] = a
        args.append(nc.dram_tensor(f"in_{name}", a.shape, mybir.dt.from_np(a.dtype), kind="ExternalInput").ap())
    out_t = nc.dram_tensor("out_0", (NB, KT, P, S), mybir.dt.float32, kind="ExternalOutput").ap()
    bass_adaln_ffn(nc, *args, out_t)
    r = run_bass_kernel_spmd(nc, [arrays], core_ids=[0])
    got = r.results[0]["out_0"]
    return got.reshape(NB, D, S).transpose(0, 2, 1)
```
